# Optimizing a Trainium2 kernel written in Bass

```python
import numpy as np
import jax
import jax.numpy as jnp

def _softmax(x, axis=-1):
    return jax.nn.softmax(x, axis=axis)

def _gelu(x):
    return jax.nn.gelu(x, approximate=True)

def _silu(x):
    return jax.nn.silu(x)

def _sigmoid(x):
    return jax.nn.sigmoid(x)

def _layernorm(x, axis=-1, eps=1e-05):
    m = jnp.mean(x, axis=axis, keepdims=True)
    v = jnp.var(x, axis=axis, keepdims=True)
    return (x - m) / jnp.sqrt(v + eps)

def _scatter_add(tgt, idx, src, axis=0):
    return tgt.at[idx].add(src)

def _segment_sum(src, seg, n):
    return jax.ops.segment_sum(src, seg, n)
kernel_name = 'mk_dlrm_tower_d1_rec_r8_039e06'

def setup_inputs(seed: int=0):
    np.random.seed(seed)
    _w = jnp.asarray

    def _rec_inputs():
        import jax
        import jax.numpy as jnp
        _tk = jax.random.key(seed)
        dense_ctx = jax.random.normal(jax.random.fold_in(_tk, 190), (512, 16), jnp.float32)
        ids = jnp.stack([jax.random.randint(jax.random.fold_in(_tk, 200 + f), (512,), 0, v, jnp.int32) for f, v in enumerate([125000, 1000, 1250, 125000, 12500, 1000, 1000, 1250, 12500, 1250, 1250, 125000, 1250, 1250, 1000, 1250, 12500, 1000, 1000, 1250, 1000, 12500, 1250, 12500, 12500, 1250, 1250, 1000, 12500, 1250, 1250, 1000])], axis=1)
        tbl_0 = 0.05 * jax.random.normal(jax.random.fold_in(_tk, 500 + 0), (125000, 64), jnp.float32)
        tbl_1 = 0.05 * jax.random.normal(jax.random.fold_in(_tk, 500 + 1), (1000, 64), jnp.float32)
        tbl_2 = 0.05 * jax.random.normal(jax.random.fold_in(_tk, 500 + 2), (1250, 64), jnp.float32)
        tbl_3 = 0.05 * jax.random.normal(jax.random.fold_in(_tk, 500 + 3), (125000, 64), jnp.float32)
        tbl_4 = 0.05 * jax.random.normal(jax.random.fold_in(_tk, 500 + 4), (12500, 64), jnp.float32)
        tbl_5 = 0.05 * jax.random.normal(jax.random.fold_in(_tk, 500 + 5), (1000, 64), jnp.float32)
        tbl_6 = 0.05 * jax.random.normal(jax.random.fold_in(_tk, 500 + 6), (1000, 64), jnp.float32)
        tbl_7 = 0.05 * jax.random.normal(jax.random.fold_in(_tk, 500 + 7), (1250, 64), jnp.float32)
        tbl_8 = 0.05 * jax.random.normal(jax.random.fold_in(_tk, 500 + 8), (12500, 64), jnp.float32)
        tbl_9 = 0.05 * jax.random.normal(jax.random.fold_in(_tk, 500 + 9), (1250, 64), jnp.float32)
        tbl_10 = 0.05 * jax.random.normal(jax.random.fold_in(_tk, 500 + 10), (1250, 64), jnp.float32)
        tbl_11 = 0.05 * jax.random.normal(jax.random.fold_in(_tk, 500 + 11), (125000, 64), jnp.float32)
        tbl_12 = 0.05 * jax.random.normal(jax.random.fold_in(_tk, 500 + 12), (1250, 64), jnp.float32)
        tbl_13 = 0.05 * jax.random.normal(jax.random.fold_in(_tk, 500 + 13), (1250, 64), jnp.float32)
        tbl_14 = 0.05 * jax.random.normal(jax.random.fold_in(_tk, 500 + 14), (1000, 64), jnp.float32)
        tbl_15 = 0.05 * jax.random.normal(jax.random.fold_in(_tk, 500 + 15), (1250, 64), jnp.float32)
        tbl_16 = 0.05 * jax.random.normal(jax.random.fold_in(_tk, 500 + 16), (12500, 64), jnp.float32)
        tbl_17 = 0.05 * jax.random.normal(jax.random.fold_in(_tk, 500 + 17), (1000, 64), jnp.float32)
        tbl_18 = 0.05 * jax.random.normal(jax.random.fold_in(_tk, 500 + 18), (1000, 64), jnp.float32)
        tbl_19 = 0.05 * jax.random.normal(jax.random.fold_in(_tk, 500 + 19), (1250, 64), jnp.float32)
        tbl_20 = 0.05 * jax.random.normal(jax.random.fold_in(_tk, 500 + 20), (1000, 64), jnp.float32)
        tbl_21 = 0.05 * jax.random.normal(jax.random.fold_in(_tk, 500 + 21), (12500, 64), jnp.float32)
        tbl_22 = 0.05 * jax.random.normal(jax.random.fold_in(_tk, 500 + 22), (1250, 64), jnp.float32)
        tbl_23 = 0.05 * jax.random.normal(jax.random.fold_in(_tk, 500 + 23), (12500, 64), jnp.float32)
        tbl_24 = 0.05 * jax.random.normal(jax.random.fold_in(_tk, 500 + 24), (12500, 64), jnp.float32)
        tbl_25 = 0.05 * jax.random.normal(jax.random.fold_in(_tk, 500 + 25), (1250, 64), jnp.float32)
        tbl_26 = 0.05 * jax.random.normal(jax.random.fold_in(_tk, 500 + 26), (1250, 64), jnp.float32)
        tbl_27 = 0.05 * jax.random.normal(jax.random.fold_in(_tk, 500 + 27), (1000, 64), jnp.float32)
        tbl_28 = 0.05 * jax.random.normal(jax.random.fold_in(_tk, 500 + 28), (12500, 64), jnp.float32)
        tbl_29 = 0.05 * jax.random.normal(jax.random.fold_in(_tk, 500 + 29), (1250, 64), jnp.float32)
        tbl_30 = 0.05 * jax.random.normal(jax.random.fold_in(_tk, 500 + 30), (1250, 64), jnp.float32)
        tbl_31 = 0.05 * jax.random.normal(jax.random.fold_in(_tk, 500 + 31), (1000, 64), jnp.float32)
        _rk = jax.random.fold_in(_tk, 7)
        W_top1 = 0.0606339 * jax.random.normal(jax.random.fold_in(_tk, 801), (272, 512), jnp.float32)
        W_top2 = 0.0441942 * jax.random.normal(jax.random.fold_in(_tk, 802), (512, 256), jnp.float32)
        W_top3 = 0.0625 * jax.random.normal(jax.random.fold_in(_tk, 803), (256, 1), jnp.float32)
        b_top1 = jnp.zeros((512,), jnp.float32)
        b_top2 = jnp.zeros((256,), jnp.float32)
        return (dense_ctx, ids, tbl_0, tbl_1, tbl_2, tbl_3, tbl_4, tbl_5, tbl_6, tbl_7, tbl_8, tbl_9, tbl_10, tbl_11, tbl_12, tbl_13, tbl_14, tbl_15, tbl_16, tbl_17, tbl_18, tbl_19, tbl_20, tbl_21, tbl_22, tbl_23, tbl_24, tbl_25, tbl_26, tbl_27, tbl_28, tbl_29, tbl_30, tbl_31, W_top1, b_top1, W_top2, b_top2, W_top3)
    dense_ctx, ids, tbl_0, tbl_1, tbl_2, tbl_3, tbl_4, tbl_5, tbl_6, tbl_7, tbl_8, tbl_9, tbl_10, tbl_11, tbl_12, tbl_13, tbl_14, tbl_15, tbl_16, tbl_17, tbl_18, tbl_19, tbl_20, tbl_21, tbl_22, tbl_23, tbl_24, tbl_25, tbl_26, tbl_27, tbl_28, tbl_29, tbl_30, tbl_31, W_top1, b_top1, W_top2, b_top2, W_top3 = _rec_inputs()

    def _L0_rec_setup():
        import jax, jax.numpy as jnp
        import numpy as np
        NUM_COLS = 32
        EMBED_DIM = 64
        LAYER_DIMS = [128, 128]
        BATCH = 1024

        def _cin_layer(X, prev_x, W, b):
            bsz, m, d = X.shape
            h = prev_x.shape[1]
            x_i = jnp.einsum('bmd,bhd->bmhd', X, prev_x).reshape(bsz, m * h, d)
            x_i = jnp.einsum('oc,bcd->bod', W, x_i) + b[None, :, None]
            return x_i
        key = jax.random.key(seed)
        k_x, k_w0, k_w1 = jax.random.split(key, 3)
        X = jax.random.normal(k_x, (BATCH, NUM_COLS, EMBED_DIM), dtype=jnp.float32)
        in0 = NUM_COLS * NUM_COLS
        in1 = NUM_COLS * LAYER_DIMS[0]
        W0 = jax.random.normal(k_w0, (LAYER_DIMS[0], in0), dtype=jnp.float32) * (1.0 / np.sqrt(in0))
        b0 = jnp.zeros((LAYER_DIMS[0],), dtype=jnp.float32)
        W1 = jax.random.normal(k_w1, (LAYER_DIMS[1], in1), dtype=jnp.float32) * (1.0 / np.sqrt(in1))
        b1 = jnp.zeros((LAYER_DIMS[1],), dtype=jnp.float32)
        return {'X': X, 'W0': W0, 'b0': b0, 'W1': W1, 'b1': b1}
    _L0_rec_all = _L0_rec_setup()
    _L0_rec_in = {k: v for k, v in _L0_rec_all.items() if k in ('W0', 'b0', 'W1', 'b1')}
    del _L0_rec_all
    return {'dense_ctx': dense_ctx, 'ids': ids, 'tbl_0': tbl_0, 'tbl_1': tbl_1, 'tbl_2': tbl_2, 'tbl_3': tbl_3, 'tbl_4': tbl_4, 'tbl_5': tbl_5, 'tbl_6': tbl_6, 'tbl_7': tbl_7, 'tbl_8': tbl_8, 'tbl_9': tbl_9, 'tbl_10': tbl_10, 'tbl_11': tbl_11, 'tbl_12': tbl_12, 'tbl_13': tbl_13, 'tbl_14': tbl_14, 'tbl_15': tbl_15, 'tbl_16': tbl_16, 'tbl_17': tbl_17, 'tbl_18': tbl_18, 'tbl_19': tbl_19, 'tbl_20': tbl_20, 'tbl_21': tbl_21, 'tbl_22': tbl_22, 'tbl_23': tbl_23, 'tbl_24': tbl_24, 'tbl_25': tbl_25, 'tbl_26': tbl_26, 'tbl_27': tbl_27, 'tbl_28': tbl_28, 'tbl_29': tbl_29, 'tbl_30': tbl_30, 'tbl_31': tbl_31, 'W_top1': W_top1, 'b_top1': b_top1, 'W_top2': W_top2, 'b_top2': b_top2, 'W_top3': W_top3, 'L0_rec_W0': _L0_rec_in['W0'], 'L0_rec_b0': _L0_rec_in['b0'], 'L0_rec_W1': _L0_rec_in['W1'], 'L0_rec_b1': _L0_rec_in['b1']}

def reference(dense_ctx, ids, tbl_0, tbl_1, tbl_2, tbl_3, tbl_4, tbl_5, tbl_6, tbl_7, tbl_8, tbl_9, tbl_10, tbl_11, tbl_12, tbl_13, tbl_14, tbl_15, tbl_16, tbl_17, tbl_18, tbl_19, tbl_20, tbl_21, tbl_22, tbl_23, tbl_24, tbl_25, tbl_26, tbl_27, tbl_28, tbl_29, tbl_30, tbl_31, W_top1, b_top1, W_top2, b_top2, W_top3, L0_rec_W0, L0_rec_b0, L0_rec_W1, L0_rec_b1):
    import jax
    import jax.numpy as jnp

    def _L0_rec_ref(X, W0, b0, W1, b1):
        import jax, jax.numpy as jnp
        import numpy as np
        NUM_COLS = 32
        EMBED_DIM = 64
        LAYER_DIMS = [128, 128]
        BATCH = 1024

        def _cin_layer(X, prev_x, W, b):
            bsz, m, d = X.shape
            h = prev_x.shape[1]
            x_i = jnp.einsum('bmd,bhd->bmhd', X, prev_x).reshape(bsz, m * h, d)
            x_i = jnp.einsum('oc,bcd->bod', W, x_i) + b[None, :, None]
            return x_i
        prev_x = X
        cin_outs = []
        for W, b in ((W0, b0), (W1, b1)):
            x_i = _cin_layer(X, prev_x, W, b)
            cin_outs.append(x_i.sum(axis=2))
            prev_x = x_i
        return jnp.concatenate(cin_outs, axis=1)
    e = jnp.stack([tbl_0[ids[:, 0]], tbl_1[ids[:, 1]], tbl_2[ids[:, 2]], tbl_3[ids[:, 3]], tbl_4[ids[:, 4]], tbl_5[ids[:, 5]], tbl_6[ids[:, 6]], tbl_7[ids[:, 7]], tbl_8[ids[:, 8]], tbl_9[ids[:, 9]], tbl_10[ids[:, 10]], tbl_11[ids[:, 11]], tbl_12[ids[:, 12]], tbl_13[ids[:, 13]], tbl_14[ids[:, 14]], tbl_15[ids[:, 15]], tbl_16[ids[:, 16]], tbl_17[ids[:, 17]], tbl_18[ids[:, 18]], tbl_19[ids[:, 19]], tbl_20[ids[:, 20]], tbl_21[ids[:, 21]], tbl_22[ids[:, 22]], tbl_23[ids[:, 23]], tbl_24[ids[:, 24]], tbl_25[ids[:, 25]], tbl_26[ids[:, 26]], tbl_27[ids[:, 27]], tbl_28[ids[:, 28]], tbl_29[ids[:, 29]], tbl_30[ids[:, 30]], tbl_31[ids[:, 31]]], axis=1)
    z = _L0_rec_ref(e, L0_rec_W0, L0_rec_b0, L0_rec_W1, L0_rec_b1)
    z = z.reshape(z.shape[0], -1)
    h = jnp.concatenate([z, dense_ctx], axis=1)
    h = jnp.maximum(h @ W_top1 + b_top1, 0.0)
    h = jnp.maximum(h @ W_top2 + b_top2, 0.0)
    y = h @ W_top3
    return y

_drawn_inputs = setup_inputs


def setup_inputs(seed=0):
    import zlib

    import numpy as np

    out = dict(_drawn_inputs(seed))
    spreads = {'b_top1': (0.0, 0.507),
     'b_top2': (0.0, 0.559),
     'L0_rec_b0': (0.0, 0.1),
     'L0_rec_b1': (0.0, 0.1)}
    factors = {'tbl_0': 8.0,
     'tbl_1': 8.0,
     'tbl_2': 8.0,
     'tbl_3': 8.0,
     'tbl_4': 8.0,
     'tbl_5': 8.0,
     'tbl_6': 8.0,
     'tbl_7': 8.0,
     'tbl_8': 8.0,
     'tbl_9': 8.0,
     'tbl_10': 8.0,
     'tbl_11': 8.0,
     'tbl_12': 8.0,
     'tbl_13': 8.0,
     'tbl_14': 8.0,
     'tbl_15': 8.0,
     'tbl_16': 8.0,
     'tbl_17': 8.0,
     'tbl_18': 8.0,
     'tbl_19': 8.0,
     'tbl_20': 8.0,
     'tbl_21': 8.0,
     'tbl_22': 8.0,
     'tbl_23': 8.0,
     'tbl_24': 8.0,
     'tbl_25': 8.0,
     'tbl_26': 8.0,
     'tbl_27': 8.0,
     'tbl_28': 8.0,
     'tbl_29': 8.0,
     'tbl_30': 8.0,
     'tbl_31': 8.0,
     'L0_rec_W0': 8.0,
     'L0_rec_W1': 5.523,
     'dense_ctx': 3.219}
    for name, (base, spread) in spreads.items():
        noise = np.random.default_rng([zlib.crc32(name.encode()), seed]).standard_normal(out[name].shape)
        drawn = base * np.exp(spread * noise) if base else spread * noise
        out[name] = jnp.asarray(drawn.astype(out[name].dtype))
    for name, factor in factors.items():
        out[name] = (out[name] * factor).astype(out[name].dtype)
    return out
```

```python
from contextlib import ExitStack

import numpy as np

import concourse.bass as bass
from concourse import mybir

B, F, DE, H = 512, 32, 64, 128
P = 128
NC = B // P
NS = 11
FAR = range(11, 17)
NFAR = len(FAR)
A_LO, A_HI = -16, 42
NA = A_HI - A_LO
MX = F + NS - 1
NT = 3
BP = P // 2
KB = 8
NK = BP // KB
XW = F + NS - 1
F1, F2 = 512, 256
DC = 16
NQ = 4


def build(nc, ids, tables, near_a, near_b, far_a, far_b, w1t, w0z, b0, b1, ctxt, wt1, bt1, wt2, bt2, wt3, out):
    f32, i32 = mybir.dt.float32, mybir.dt.int32
    ALU, ACT = mybir.AluOpType, mybir.ActivationFunctionType
    X_AX = mybir.AxisListType.X

    with ExitStack() as ctx:
        def sb(name, shape, dt=f32):
            return ctx.enter_context(nc.sbuf_tensor(name, shape, dt))

        def sem(name):
            return ctx.enter_context(nc.semaphore(name))

        xt_n, xb_n = BP * XW, BP * 2 * F
        t_n, pp_n = F * P, KB * P
        T_AT = xb_n + 2 * xt_n
        PP_AT = T_AT + NT * t_n
        MAIN_N = PP_AT + 4 * pp_n
        vf_n, e_n = MX * NFAR * NA, NS * 11 * F
        VF_AT = xb_n + xt_n
        E_AT = VF_AT + vf_n
        assert E_AT + e_n <= MAIN_N
        main = sb("main", [P, MAIN_N])
        XB = main[:, 0:xb_n].rearrange("p (b m) -> p b m", m=2 * F)
        XT = main[:, xb_n:T_AT].rearrange("p (c b m) -> p c b m", c=2, m=XW)
        T = main[:, T_AT:PP_AT].rearrange("p (t h m b) -> p t h m b", t=NT, h=2, m=F)
        PP = main[:, PP_AT:MAIN_N].rearrange("p (s b n) -> p s b n", s=4, b=KB)
        VF = main[:, VF_AT:E_AT].rearrange("p (m n) -> p m n", m=MX)
        EV = main[:, E_AT:E_AT + e_n].rearrange("p (s r j) -> p s r j", s=NS, r=11)

        def in_main(at, dims):
            return bass.AP(main[:, 0:1].tensor, at, [[MAIN_N, P]] + dims)

        w1_n, ring_n = F * H, 4 * NT * P
        na_n, fa_n, fb_n = NS * F, NFAR * NA, (NFAR - 1) * NA
        early = np.cumsum([0, w1_n, ring_n, na_n, na_n, fa_n, fb_n]).tolist()
        late = np.cumsum([0, F * 2 * 32, 8 * H, 2 * F1, F1, 4 * F2, 2 * B, B]).tolist()
        side = sb("side", [P, max(early[-1], late[-1])])
        W1T = side[:, early[0]:early[1]].rearrange("p (m o) -> p m o", m=F)
        RING = side[:, early[1]:early[2]].rearrange("p (s n) -> p s n", s=4)
        NEAR = side[:, early[2]:early[3]]
        NEAR_B = side[:, early[3]:early[4]]
        FARP = side[:, early[4]:early[5]]
        FAR_B = side[:, early[5]:early[6]]
        GQ = side[:, 0:8 * P].rearrange("p (h m b) -> p h m b", h=2, m=8)
        W0Z = side[:, late[1]:late[2]].rearrange("p (m o) -> p m o", m=8)
        WT1 = side[:, late[2]:late[3]].rearrange("p (k n) -> p k n", k=2)
        WT1C = side[0:DC, late[3]:late[4]]
        WT2 = side[:, late[4]:late[5]].rearrange("p (k n) -> p k n", k=4)
        ZT = side[:, late[5]:late[6]].rearrange("p (z b) -> p z b", z=2)
        CT = side[0:DC, late[6]:late[7]]

        DT = sb("DT", [P, F, NT, H])
        XG = sb("XG", [P, F + 1, DE])
        H1 = XG[:, 0:F, :].rearrange("p f d -> p (f d)").rearrange("p (k b) -> p k b", k=4)
        H2 = main[:, 0:2 * B].rearrange("p (k b) -> p k b", k=2)
        Y = sb("Y", [1, B])
        ident = sb("ident", [P, P])
        idx = sb("idx", [P, NC, F], i32)
        S = sb("S", [P, F])
        ST = sb("ST", [F, P])
        LS = sb("LS", [P, F])
        LT = sb("LT", [F, H])
        b0s, b1s = sb("b0s", [P, 1]), sb("b1s", [P, 1])
        b64 = sb("b64", [P, 2])
        bt1s, bt2s, wt3s = sb("bt1s", [P, 4]), sb("bt2s", [P, 2]), sb("wt3s", [P, 2])
        bank = [ctx.enter_context(nc.psum_tensor(f"bank{i}", [P, 512], f32)) for i in range(8)]

        ids_in, pairs_in, small_in, late_in = sem("ids_in"), sem("pairs_in"), sem("small_in"), sem("late_in")
        w1_in = [sem(f"w1_in{i}") for i in range(4)]
        id_zero, id_done = sem("id_zero"), sem("id_done")
        gathered = [sem(f"gathered{i}") for i in range(NQ)]
        pairs_sum = sem("pairs_sum")
        zeroed = sem("zeroed")
        far_mm, far_ev, far_dup = sem("far_mm"), sem("far_ev"), sem("far_dup")
        moved = sem("moved")
        near_mm, near_ev, d_ready = sem("near_mm"), sem("near_ev"), sem("d_ready")
        dt_mm, dt_ev_act, dt_ev_dve = sem("dt_mm"), sem("dt_ev_act"), sem("dt_ev_dve")
        lin_mm, lin_ev = sem("lin_mm"), sem("lin_ev")
        xt_mm, xt_ev = sem("xt_mm"), sem("xt_ev")
        xt_full = sem("xt_full")
        xb_done = sem("xb_done")
        s_red, st_mm, st_ev = sem("s_red"), sem("st_mm"), sem("st_ev")
        pp_ready = sem("pp_ready")
        t_mm, t_ev = sem("t_mm"), sem("t_ev")
        gq_in = sem("gq_in")
        z1_mm, z1_ev, z0_mm, z0_ev = sem("z1_mm"), sem("z1_ev"), sem("z0_mm"), sem("z0_ev")
        h1_mm, h1_ev, h2_mm, h2_ev = sem("h1_mm"), sem("h1_ev"), sem("h2_mm"), sem("h2_ev")
        y_mm, y_ev, out_done = sem("y_mm"), sem("y_ev"), sem("out_done")

        def par(c):
            return c % 2

        def at(view, i):
            return view[:, i] if isinstance(i, int) else view[:, bass.ds(i, 1)].squeeze(1)

        block = ctx.enter_context(nc.Block())

        @block.sync
        def _(sp):
            sp.dma_start(idx[:, :, :], ids).then_inc(ids_in, 16)
            sp.dma_start(FARP, far_a).then_inc(pairs_in, 16)
            sp.dma_start(FAR_B, far_b).then_inc(pairs_in, 16)
            for i in range(4):
                sp.dma_start(W1T[:, 8 * i:8 * i + 8, :], w1t[:, 8 * i:8 * i + 8, :]).then_inc(w1_in[i], 16)
            for dst, src in ((NEAR, near_a), (NEAR_B, near_b)):
                sp.dma_start(dst, src).then_inc(pairs_in, 16)
            for dst, src in ((b0s[:, :], b0), (b1s[:, :], b1), (bt1s[:, :], bt1), (bt2s[:, :], bt2), (wt3s[:, :], wt3)):
                sp.dma_start(dst, src).then_inc(small_in, 16)
            sp.wait_ge(dt_mm, F)
            for dst, src in ((W0Z, w0z), (CT, ctxt), (WT1, wt1[0:2 * P, :].rearrange("(k p) n -> p k n", p=P)),
                             (WT1C, wt1[2 * P:, :]), (WT2, wt2.rearrange("(k p) n -> p k n", p=P))):
                sp.dma_start(dst, src).then_inc(late_in, 16)
            with sp.Fori(0, NC) as c:
                sp.wait_ge(t_ev, 24 * c + 24)
                for q in range(4):
                    sp.dma_start(GQ[32 * q:32 * q + 32, :, :, :],
                                 T[96:128, 2, :, 8 * q:8 * q + 8, :]).then_inc(gq_in, 16)
            sp.wait_ge(y_ev, 1)
            sp.dma_start(out.rearrange("b o -> o b"), Y[:, :]).then_inc(out_done, 16)
            sp.wait_ge(out_done, 16)

        @block.gpsimd
        def _(pool):
            pool.memset(ident[:, :], 0.0).then_inc(id_zero, 1)
            pool.wait_ge(id_zero, 1)
            pool.affine_select(out=ident[:, :], in_=ident[:, :], compare_op=ALU.not_equal, fill=1.0, base=0,
                               pattern=[[-1, P]], channel_multiplier=1).then_inc(id_done, 1)
            pool.wait_ge(ids_in, 16)
            for c in range(NC):
                if c:
                    pool.wait_ge(s_red, 2 * c)
                for f in range(F):
                    if c and f % 8 == 0:
                        pool.wait_ge(gathered[f // 8], 128 * c)
                    if c and f % 4 == 0:
                        pool.wait_ge(xt_mm, 8 * (c - 1) + f // 4 + 1)
                    pool.indirect_dma_start(
                        out=XG[:, f, :], out_offset=None, in_=tables[f],
                        in_offset=bass.IndirectOffsetOnAxis(ap=idx[:, c, f:f + 1], axis=0),
                    ).then_inc(gathered[f // 8], 16)

        @block.vector
        def _(dve):
            v = nc.vector
            v.memset(RING[:, :, NS * F:], 0.0).then_inc(zeroed, 1)
            v.memset(XB[0:64, :, F:2 * F], 0.0).then_inc(zeroed, 1)
            v.memset(XB[64:128, :, 0:F], 0.0).then_inc(zeroed, 1)
            dve.wait_ge(pairs_in, 64)
            v.tensor_tensor(FARP[:, 0:fb_n], FARP[:, 0:fb_n], FAR_B, ALU.add).then_inc(pairs_sum, 1)
            v.tensor_tensor(NEAR[:, F:], NEAR[:, F:], NEAR_B[:, F:], ALU.add).then_inc(pairs_sum, 1)
            dve.wait_ge(small_in, 80)
            v.tensor_scalar_mul(b64[:, 0:1], b0s[:, :], float(DE)).then_inc(pairs_sum, 1)
            v.tensor_scalar_mul(b64[:, 1:2], b1s[:, :], float(DE)).then_inc(pairs_sum, 1)

            dve.wait_ge(far_ev, F)
            v.tensor_copy(VF[:, F:MX, :], VF[:, 0:MX - F, :]).then_inc(far_dup, 1)
            dve.wait_ge(far_dup, 1)

            row = NFAR * NA
            steps = [0]

            def moved_step(ins):
                steps[0] += 1
                ins.then_inc(moved, 1)

            moved_step(v.tensor_copy(EV[:, :, 0:6, :], in_main(VF_AT + 16, [[row, NS], [NA, 6], [row + 1, F]])))
            moved_step(v.tensor_copy(EV[:, :, 6:11, :], in_main(VF_AT + 4 * NA + 1, [[row, NS], [1 - NA, 5], [row + 1, F]])))
            dve.wait_ge(moved, steps[0])
            moved_step(v.tensor_tensor(EV[:, :, 5, :], EV[:, :, 5, :],
                                       in_main(VF_AT + 5 * NA, [[row, NS], [row + 1, F]]), ALU.add))
            for s in range(1, 6):
                n = 6 - s
                dve.wait_ge(moved, steps[0])
                e = in_main(E_AT + s * 11 * F + 10 * F, [[-F, n], [1, F]])
                moved_step(v.tensor_tensor(e, e, in_main(VF_AT + s * NA + 5, [[NA - 1, n], [row + 1, F]]), ALU.add))
            for s in range(1, NS):
                n = min(16, 21 - s) - 10
                dve.wait_ge(moved, steps[0])
                e = EV[:, s, s:s + n, :]
                moved_step(v.tensor_tensor(e, e, in_main(VF_AT + s + 16, [[NA, n], [row + 1, F]]), ALU.add))
            dve.wait_ge(moved, steps[0])

            def add_moved(m):
                dve.wait_ge(near_ev, m + 1)
                parts = []
                if m >= 11:
                    j0 = max(0, m - 21)
                    parts.append((j0, m - 10 - j0, m - j0 - 11))
                if m + 11 < F:
                    parts.append((m + 11, min(F - 1, m + 21) - m - 10, 10))
                for j0, n, r in parts:
                    d = RING[:, m % 4, 0:NS * F].rearrange("p (s j) -> p s j", s=NS)[:, :, j0:j0 + n]
                    last = v.tensor_tensor(d, d, in_main(E_AT + r * F + j0, [[11 * F, NS], [1 - F, n]]), ALU.add)
                last.then_inc(d_ready, 1)

            def sum_rows(c, wait_st):
                for q in range(NQ):
                    dve.wait_ge(gathered[q], 128 * (c + 1))
                if wait_st:
                    dve.wait_ge(st_mm, c)
                v.tensor_reduce(S[:, :], XG[:, 0:F, :], X_AX, ALU.add).then_inc(s_red, 1)
                v.tensor_copy(XG[:, F, :], XG[:, 0, :]).then_inc(s_red, 1)

            for m in range(F + 3):
                if m < F:
                    add_moved(m)
                if m == 24:
                    sum_rows(0, False)
                if m >= 3 and (m - 3) % 2:
                    dve.wait_ge(dt_mm, m - 2)
                    v.tensor_copy(DT[:, m - 3, :, :], bank[7][:, 0:NT * H]).then_inc(dt_ev_dve, 1)

            def repeat(c):
                dve.wait_ge(xt_ev, 8 * c + 8)
                xt = at(XT, par(c))
                v.tensor_scalar_mul(xt[:, :, F:XW], xt[:, :, 0:XW - F], 1.0).then_inc(xt_full, 1)
                dve.wait_ge(xt_full, c + 1)

            def spread(c, wait_mm):
                if wait_mm:
                    dve.wait_ge(t_mm, 24 * c)
                xt = at(XT, par(c))
                v.tensor_scalar_mul(XB[0:64, :, 0:F], xt[0:64, :, 0:F], 1.0).then_inc(xb_done, 1)
                v.tensor_scalar_mul(XB[64:128, :, F:2 * F], xt[64:128, :, 0:F], 1.0).then_inc(xb_done, 1)

            def xt_pairs(c, t, k, n):
                base = XT[:, c, KB * k:KB * k + KB, 4 * t:4 * t + F] if isinstance(c, int) else \
                    XT[:, bass.ds(c, 1), KB * k:KB * k + KB, 4 * t:4 * t + F].squeeze(1)
                a = base.ap
                return bass.AP(base.tensor, base.offset, [list(a[0]), list(a[-2]), [1, n], [1, F]])

            def products(c, t, waits=True):
                n = 3 if t == 2 else 4
                for k in range(NK):
                    if waits or k >= 4:
                        dve.wait_ge(t_mm, 24 * c + 8 * t + k - 3)
                    pp = PP[:, k % 4, :, :]
                    if t == 2:
                        v.tensor_scalar_mul(pp[:, :, n * F:], at(XT, par(c))[:, KB * k:KB * k + KB, 0:F], 1.0)
                    x = at(XT, par(c))[:, KB * k:KB * k + KB, 0:F].unsqueeze(2).to_broadcast([P, KB, n, F])
                    v.tensor_tensor(pp[:, :, 0:n * F].rearrange("p b (s j) -> p b s j", s=n), x,
                                    xt_pairs(par(c), t, k, n), ALU.mult).then_inc(pp_ready, 1)
                    if t == 0 and k == 1:
                        spread(c, waits)
                    if t == 2 and k == 3 and not (isinstance(c, int) and c == NC - 1):
                        sum_rows(c + 1, True)

            repeat(0)
            products(0, 0, waits=False)
            with dve.Fori(0, NC - 1) as c:
                products(c, 1)
                products(c, 2)
                repeat(c + 1)
                products(c + 1, 0)
            products(NC - 1, 1)
            products(NC - 1, 2)

            for k in (1, 3):
                dve.wait_ge(h1_mm, k + 1)
                v.tensor_scalar(H1[:, k, :], bank[k][:, :], bt1s[:, k:k + 1], 0.0, ALU.add, ALU.max).then_inc(h1_ev, 1)
            dve.wait_ge(h2_mm, 2)
            v.tensor_scalar(H2[:, 1, :], bank[5][:, :], bt2s[:, 1:2], 0.0, ALU.add, ALU.max).then_inc(h2_ev, 1)

        @block.scalar
        def _(act):
            a = nc.scalar

            def copy(dst, src):
                return a.activation(dst, src, ACT.Copy)

            for m in range(F):
                act.wait_ge(far_mm, m + 1)
                copy(VF[:, m, :], bank[m % 4][:, 0:fa_n]).then_inc(far_ev, 1)
            act.wait_ge(lin_mm, 1)
            copy(LS[:, :], bank[6][:, 0:F]).then_inc(lin_ev, 1)
            act.wait_ge(lin_mm, 2)
            copy(LT[:, :], bank[6][0:F, 0:H]).then_inc(lin_ev, 1)

            def x_out(c, g, banks):
                act.wait_ge(xt_mm, 8 * c + g + 1)
                src = banks[g % 2][:, :].rearrange("p (m b) -> p b m", m=4)
                xt = at(XT, par(c))
                copy(xt[0:64, :, 4 * g:4 * g + 4], src[0:64, 0:BP, :])
                n = 4 if g < 7 else 3
                last = copy(xt[64:128, :, 4 * g + 1:4 * g + 1 + n], src[64:128, BP:P, 0:n])
                if g == 7:
                    last = copy(xt[64:128, :, 0:1], src[64:128, BP:P, 3:4])
                last.then_inc(xt_ev, 1)

            for m in range(F + 3):
                if m < F:
                    act.wait_ge(near_mm, m + 1)
                    if m == 0:
                        act.wait_ge(zeroed, 1)
                    if m >= 4:
                        act.wait_ge(dt_mm, m - 3)
                    copy(RING[:, m % 4, 0:NS * F], bank[4 + m % 2][:, 0:NS * F]).then_inc(near_ev, 1)
                if m >= 3 and (m - 3) % 2 == 0:
                    act.wait_ge(dt_mm, m - 2)
                    copy(DT[:, m - 3, :, :], bank[6][:, 0:NT * H]).then_inc(dt_ev_act, 1)
                if 16 <= m < F and m % 2 == 0:
                    x_out(0, (m - 16) // 2, (bank[2], bank[3]))

            def moments_out(c, t):
                for k in range(NK):
                    act.wait_ge(t_mm, 24 * c + 8 * t + k + 1)
                    dst = T[:, t].rearrange("p h m b -> p (h m) b")[:, :, KB * k:KB * k + KB]
                    copy(dst, bank[k % 4][:, :].rearrange("p (b n) -> p n b", b=KB)).then_inc(t_ev, 1)
                    if t == 2 and k < 4 and not (isinstance(c, int) and c == NC - 1):
                        x_out(c + 1, 2 * k, (bank[4], bank[5]))
                        x_out(c + 1, 2 * k + 1, (bank[4], bank[5]))
                    if t == 1 and k == 5:
                        act.wait_ge(st_mm, c + 1)
                        copy(ST[:, :], bank[7][0:F, 0:P]).then_inc(st_ev, 1)

            def z_out(c):
                act.wait_ge(z1_mm, c + 1)
                a.activation(at(ZT.rearrange("p z (c b) -> p c z b", c=NC), c)[:, 1, :], bank[6][:, 0:P],
                             ACT.Identity, bias=b64[:, 1:2]).then_inc(z1_ev, 1)
                act.wait_ge(z0_mm, c + 1)
                a.activation(at(ZT.rearrange("p z (c b) -> p c z b", c=NC), c)[:, 0, :], bank[7][:, P:2 * P],
                             ACT.Identity, bias=b64[:, 0:1]).then_inc(z0_ev, 1)

            moments_out(0, 0)
            act.wait_ge(pairs_sum, 4)
            with act.Fori(0, NC - 1) as c:
                moments_out(c, 1)
                moments_out(c, 2)
                moments_out(c + 1, 0)
                z_out(c)
                act.wait_ge(gq_in, 64 * c + 64)
            moments_out(NC - 1, 1)
            moments_out(NC - 1, 2)
            z_out(NC - 1)

            for k in (0, 2):
                act.wait_ge(h1_mm, k + 1)
                a.activation(H1[:, k, :], bank[k][:, :], ACT.Relu, bias=bt1s[:, k:k + 1]).then_inc(h1_ev, 1)
            act.wait_ge(h2_mm, 1)
            a.activation(H2[:, 0, :], bank[4][:, :], ACT.Relu, bias=bt2s[:, 0:1]).then_inc(h2_ev, 1)
            act.wait_ge(y_mm, 1)
            copy(Y[:, :], bank[6][0:1, :]).then_inc(y_ev, 1)

        @block.tensor
        def _(pe):
            mm = nc.tensor.matmul

            for m in range(F):
                if m == 0:
                    pe.wait_ge(pairs_sum, 1)
                if m % 8 == 0:
                    pe.wait_ge(w1_in[m // 8], 16)
                if m >= 4:
                    pe.wait_ge(far_ev, m - 3)
                mm(bank[m % 4][:, 0:fa_n], W1T[:, m, :], FARP, start=True, stop=True).then_inc(far_mm, 1)
            pe.wait_ge(small_in, 80)
            for m in range(F):
                last = mm(bank[6][:, m:m + 1], W1T[:, m, :], b0s[:, :], start=True, stop=True)
            last.then_inc(lin_mm, 1)
            pe.wait_ge(lin_ev, 1)
            pe.wait_ge(id_done, 1)
            mm(bank[6][0:F, 0:H], LS[:, :], ident[:, :], start=True, stop=True).then_inc(lin_mm, 1)

            def x_group(c, g, banks):
                if g == 0:
                    pe.wait_ge(gathered[0], 128 * (c + 1))
                if g % 2 and g < 7:
                    pe.wait_ge(gathered[g // 2 + 1], 128 * (c + 1))
                if g == 7:
                    pe.wait_ge(s_red, 2 * c + 2)
                if not (isinstance(c, int) and c == 0 and g < 2):
                    pe.wait_ge(xt_ev, 8 * c + g - 1)
                for i in range(4):
                    last = nc.tensor.transpose(banks[g % 2][:, i * P:(i + 1) * P],
                                               XG[:, 4 * g + i:4 * g + i + 2, :].rearrange("p f d -> p (f d)"), ident[:, :])
                last.then_inc(xt_mm, 1)

            pe.wait_ge(pairs_sum, 2)
            pe.wait_ge(lin_ev, 2)
            for m in range(F + 2):
                if m < F:
                    if m >= 2:
                        pe.wait_ge(near_ev, m - 1)
                    mm(bank[4 + m % 2][:, 0:na_n], W1T[:, m, :], NEAR, start=True, stop=True).then_inc(near_mm, 1)
                if m >= 2:
                    pe.wait_ge(d_ready, m - 1)
                    n = m - 2
                    if n >= 2:
                        pe.wait_ge(dt_ev_dve if n % 2 else dt_ev_act, n // 2)
                    for t in range(NT):
                        last = nc.tensor.transpose(bank[6 + n % 2][:, t * P:(t + 1) * P],
                                                   RING[:, n % 4, t * P:(t + 1) * P], ident[:, :])
                    last.then_inc(dt_mm, 1)
                if m == 16:
                    pe.wait_ge(far_ev, F)
                if 16 <= m < F and m % 2 == 0:
                    x_group(0, (m - 16) // 2, (bank[2], bank[3]))
            pe.wait_ge(dt_ev_act, F // 2)
            pe.wait_ge(dt_ev_dve, F // 2)

            def moments(c, t, k, waits=True):
                pe.wait_ge(pp_ready, 24 * c + 8 * t + k + 1)
                if t == 0 and k == 0:
                    pe.wait_ge(xb_done, 2 * c + 2)
                    if not waits:
                        pe.wait_ge(zeroed, 3)
                if waits or k >= 4:
                    pe.wait_ge(t_ev, 24 * c + 8 * t + k - 3)
                for i in range(KB):
                    last = mm(bank[k % 4][:, 2 * F * i:2 * F * (i + 1)], PP[:, k % 4, i, :],
                              XB[:, KB * k + i, :], start=True, stop=True)
                last.then_inc(t_mm, 1)

            def contract(c, t, k):
                if k == 0:
                    pe.wait_ge(t_ev, 24 * c + 8 * t + 8 + (t == 0))
                rows = 96 if t == 2 else P
                z = bank[6][:, 0:P].rearrange("p (h b) -> p h b", h=2)
                for m in range(4 * k, 4 * k + 4):
                    mm(z, DT[0:rows, m, t, :], T[0:rows, t, :, m, :],
                       start=t == 0 and m == 0, stop=False)
                if k == NK - 1 and t == 2:
                    pe.wait_ge(st_ev, c + 1)
                    mm(bank[6][:, 0:P], LT[:, :], ST[:, :], start=False, stop=True).then_inc(z1_mm, 1)

            def gram(c):
                pe.wait_ge(gq_in, 64 * c + 64)
                z = bank[7][:, P:2 * P].rearrange("p (h b) -> p h b", h=2)
                for m in range(8):
                    last = mm(z, W0Z[:, m, :], GQ[:, :, m, :], start=m == 0, stop=m == 7)
                last.then_inc(z0_mm, 1)

            def s_rows(c):
                pe.wait_ge(s_red, 2 * c + 1)
                mm(bank[7][0:F, 0:P], S[:, :], ident[:, :], start=True, stop=True).then_inc(st_mm, 1)

            def unit_1(c):
                for k in range(NK):
                    moments(c, 1, k)
                    if k:
                        contract(c, 0, k - 1)
                    if k == 4:
                        s_rows(c)
                contract(c, 0, NK - 1)

            for k in range(NK):
                moments(0, 0, k, waits=False)
            pe.wait_ge(late_in, 80)
            with pe.Fori(0, NC - 1) as c:
                unit_1(c)
                for k in range(NK):
                    moments(c, 2, k)
                    if k < 4:
                        x_group(c + 1, 2 * k, (bank[4], bank[5]))
                        x_group(c + 1, 2 * k + 1, (bank[4], bank[5]))
                    if k >= 2:
                        contract(c, 1, k - 2)
                contract(c, 1, NK - 2)
                contract(c, 1, NK - 1)
                for k in range(NK):
                    moments(c + 1, 0, k)
                    contract(c, 2, k)
                gram(c)
            c = NC - 1
            unit_1(c)
            for k in range(NK):
                moments(c, 2, k)
                contract(c, 1, k)
            for k in range(NK):
                contract(c, 2, k)
            gram(c)

            pe.wait_ge(z1_ev, NC)
            pe.wait_ge(z0_ev, NC)
            for k in range(4):
                cols = slice(k * P, (k + 1) * P)
                mm(bank[k][:, :], WT1[:, 0, cols], ZT[:, 0, :], start=True, stop=False)
                mm(bank[k][:, :], WT1[:, 1, cols], ZT[:, 1, :], start=False, stop=False)
                mm(bank[k][:, :], WT1C[:, cols], CT, start=False, stop=True).then_inc(h1_mm, 1)
            pe.wait_ge(h1_ev, 4)
            for n in range(2):
                for k in range(4):
                    last = mm(bank[4 + n][:, :], WT2[:, k, n * P:(n + 1) * P], H1[:, k, :], start=k == 0, stop=k == 3)
                last.then_inc(h2_mm, 1)
            pe.wait_ge(h2_ev, 2)
            for k in range(2):
                last = mm(bank[6][0:1, :], wt3s[:, k:k + 1], H2[:, k, :], start=k == 0, stop=k == 1)
            last.then_inc(y_mm, 1)


def kernel(**inputs):
    import concourse.bacc as bacc
    from concourse.bass_utils import run_bass_kernel_spmd

    a = {n: np.asarray(x) for n, x in inputs.items()}
    w0 = a["L0_rec_W0"].reshape(H, F, F)
    j = np.arange(F)
    at_far = np.arange(A_LO, A_HI)
    near_a = np.stack([w0[:, j, (j + s) % F] for s in range(NS)], 1)
    near_b = np.stack([w0[:, (j + s) % F, j] for s in range(NS)], 1)
    far_a = np.stack([w0[:, at_far % F, (at_far + s) % F] for s in FAR], 1)
    far_b = np.stack([w0[:, (at_far + s) % F, at_far % F] for s in FAR if s < F // 2], 1)
    arrays = {
        "ids": a["ids"].reshape(NC, P, F).transpose(1, 0, 2),
        **{f"tbl_{f}": a[f"tbl_{f}"] for f in range(F)},
        "near_a": near_a.reshape(H, -1), "near_b": near_b.reshape(H, -1),
        "far_a": far_a.reshape(H, -1), "far_b": far_b.reshape(H, -1),
        "w1t": a["L0_rec_W1"].reshape(H, F, H).transpose(2, 1, 0),
        "w0z": w0.reshape(H, F, 4, 8).transpose(2, 1, 3, 0).reshape(P, 8, H),
        "b0": a["L0_rec_b0"].reshape(H, 1), "b1": a["L0_rec_b1"].reshape(H, 1),
        "ctxt": a["dense_ctx"].T, "wt1": a["W_top1"], "bt1": a["b_top1"].reshape(4, P).T,
        "wt2": a["W_top2"], "bt2": a["b_top2"].reshape(2, P).T, "wt3": a["W_top3"].reshape(2, P).T,
    }
    arrays = {n: np.ascontiguousarray(x) for n, x in arrays.items()}
    nc = bacc.Bacc("TRN2", target_bir_lowering=False, num_devices=1)
    d = {n: nc.dram_tensor(f"in_{n}", x.shape, mybir.dt.from_np(x.dtype), kind="ExternalInput").ap()
         for n, x in arrays.items()}
    out = nc.dram_tensor("out", (B, 1), mybir.dt.float32, kind="ExternalOutput").ap()
    build(nc, d["ids"], [d[f"tbl_{f}"] for f in range(F)], d["near_a"], d["near_b"], d["far_a"], d["far_b"],
          d["w1t"], d["w0z"], d["b0"], d["b1"], d["ctxt"], d["wt1"], d["bt1"], d["wt2"], d["bt2"], d["wt3"], out)
    r = run_bass_kernel_spmd(nc, [{f"in_{n}": x for n, x in arrays.items()}], core_ids=[0])
    return r.results[0]["out"]
```

```python
from contextlib import ExitStack

import numpy as np

import concourse.bass as bass
from concourse import mybir

B, F, DE, H = 512, 32, 64, 128
P = 128
NC = B // P
HF = F // 2
NS = HF // 2
NN = 2 * (NS * HF + NS)
NX = HF * HF
BP = P // 2
KB = 4
NK = BP // KB
CL = 2 * P
CX = CL + F
NP = CX + F
XW = HF + NS
PPS = 3
F1, F2 = 512, 256
DC = 16
NQ = 4
NG = 8
XK = 7
NDT = F // 2 + 2


def bank7_uses():
    uses = [("x", 0, g) for g in range(NG)]
    for c in range(NC):
        for k in range(NK):
            if k:
                uses.append(("t2", c, k - 1))
            if k == 2:
                uses.append(("s", c, 0))
            if c < NC - 1 and XK <= k < XK + NG:
                uses.append(("x", c + 1, k - XK))
        uses.append(("t2", c, NK - 1))
        if c:
            uses.append(("z0", c - 1, 0))
    uses.append(("z0", NC - 1, 0))
    return {u: n for n, u in enumerate(uses)}


def build(nc, ids, tables, near_a, near_b, cross_a, cross_b, w1t, w0z, b0, b1, ctxt, wt1, bt1, wt2, bt2, wt3, out):
    f32, i32 = mybir.dt.float32, mybir.dt.int32
    ALU, ACT = mybir.AluOpType, mybir.ActivationFunctionType
    AX = mybir.AxisListType

    with ExitStack() as ctx:
        def sb(name, shape, dt=f32):
            return ctx.enter_context(nc.sbuf_tensor(name, shape, dt))

        def sem(name):
            return ctx.enter_context(nc.semaphore(name))

        xt_n, t_n, t2_n = BP * 2 * XW, 2 * F * P, 2 * F * F
        T_AT = 2 * xt_n
        T2_AT = T_AT + 2 * t_n
        MAIN_N = T2_AT + t2_n
        F_AT = xt_n
        D_AT = F_AT + F * NX
        W1_AT = D_AT + F * NN
        assert W1_AT + F * H <= MAIN_N
        main = sb("main", [P, MAIN_N])
        XT = main[:, 0:T_AT].rearrange("p (c b m) -> p c b m", c=2, m=2 * XW)
        T = main[:, T_AT:T2_AT].rearrange("p (c t n b) -> p c t n b", c=2, t=2, b=BP)
        T2 = main[:, T2_AT:MAIN_N].rearrange("p (n b) -> p n b", b=BP // 2)
        FX = main[:, F_AT:D_AT].rearrange("p (m n) -> p m n", m=F)
        D = main[:, D_AT:W1_AT].rearrange("p (m n) -> p m n", m=F)
        W1T = main[:, W1_AT:W1_AT + F * H].rearrange("p (m o) -> p m o", m=F)
        H2 = main[:, 0:2 * B].rearrange("p (k b) -> p k b", k=2)
        WT1 = main[:, T_AT:T_AT + 2 * F1].rearrange("p (k n) -> p k n", k=2)
        WT1C = main[0:DC, T_AT + 2 * F1:T_AT + 3 * F1]
        WT2 = main[:, T_AT + 3 * F1:T_AT + 3 * F1 + 4 * F2].rearrange("p (k n) -> p k n", k=4)

        def in_main(at, dims):
            return bass.AP(main[:, 0:1].tensor, at, [[MAIN_N, P]] + dims)

        XB = sb("XB", [P, BP, 2 * F])
        PP = sb("PP", [P, PPS, KB, NP])
        U = sb("U", [P, 2, 2 * CL])
        U2 = sb("U2", [P, 2, 2 * 2 * F])
        DT = sb("DT", [P, F, 2, H])
        DLT = sb("DLT", [P, 8, H])
        GL = sb("GL", [P, 4, 8, F])
        GG = sb("GG", [P, 4, 8, F])
        W0Z = sb("W0Z", [P, 8, H])
        ZT = sb("ZT", [P, 2, B])
        XG = sb("XG", [P, F + 1, DE])
        H1 = XG[:, 0:F, :].rearrange("p f d -> p (f d)").rearrange("p (k b) -> p k b", k=4)
        DL = GL[:, :, :, :].rearrange("p a m b -> p (a m b)").rearrange("p (m q r) -> p m q r", m=8, q=4)
        gg = GG[:, :, :, :].rearrange("p a m b -> p (a m b)")
        NEAR, NEAR_B = gg[:, 0:NN], gg[:, NN:2 * NN]
        zt = ZT[:, :, :].rearrange("p z b -> p (z b)")
        CROSS, CROSS_B = zt[:, 0:NX], zt[:, NX:2 * NX]
        CTX = sb("CTX", [DC, B])
        Y = sb("Y", [1, B])
        ident = sb("ident", [P, P])
        idx = sb("idx", [P, NC, F], i32)
        S = sb("S", [P, F])
        ST = sb("ST", [F, P])
        LS = sb("LS", [P, F])
        LT = sb("LT", [F, H])
        b0s, b1s = sb("b0s", [P, 1]), sb("b1s", [P, 1])
        b64 = sb("b64", [P, 2])
        bt1s, bt2s, wt3s = sb("bt1s", [P, 4]), sb("bt2s", [P, 2]), sb("wt3s", [P, 2])
        psum = ctx.enter_context(nc.psum_tensor("psum", [P, 8, 512], f32))
        bank = [psum[:, i, :] for i in range(8)]

        ids_in, cross_in, near_in, small_in = sem("ids_in"), sem("cross_in"), sem("near_in"), sem("small_in")
        w1_in = [sem(f"w1_in{i}") for i in range(4)]
        w0z_in, mlp_in = sem("w0z_in"), sem("mlp_in")
        id_zero, id_done = sem("id_zero"), sem("id_done")
        gathered = [sem(f"gathered{i}") for i in range(NQ)]
        zeroed = sem("zeroed")
        cross_sum, near_sum, b_sum = sem("cross_sum"), sem("near_sum"), sem("b_sum")
        v_mm, v_ev = sem("v_mm"), sem("v_ev")
        moved, left = sem("moved"), sem("left")
        dt_mm = sem("dt_mm")
        dt_act, dt_dve = sem("dt_act"), sem("dt_dve")
        lin_mm, lin_ev = sem("lin_mm"), sem("lin_ev")
        x_mm, st_mm, st_ev = sem("x_mm"), sem("st_mm"), sem("st_ev")
        b7_ev = sem("b7_ev")
        xt_full, xb_done, s_red = sem("xt_full"), sem("xb_done"), sem("s_red")
        pp_ready = sem("pp_ready")
        t_mm, u_ev = sem("t_mm"), sem("u_ev")
        tr_mm, tr_ev = sem("tr_mm"), sem("tr_ev")
        g_in = sem("g_in")
        z1_mm, z1_ev, z0_mm, z0_ev = sem("z1_mm"), sem("z1_ev"), sem("z0_mm"), sem("z0_ev")
        h1_mm, h1_ev, h2_mm, h2_ev = sem("h1_mm"), sem("h1_ev"), sem("h2_mm"), sem("h2_ev")
        y_mm, y_ev, out_done = sem("y_mm"), sem("y_ev"), sem("out_done")

        use7 = bank7_uses()

        def dt_engine(n):
            if n < 8:
                return dt_act, n + 1
            return (dt_dve, (n - 9) // 2 + 1) if n % 2 else (dt_act, 8 + (n - 8) // 2 + 1)

        block = ctx.enter_context(nc.Block())

        @block.sync
        def _(sp):
            sp.dma_start(idx[:, :, :], ids).then_inc(ids_in, 16)
            sp.dma_start(CROSS, cross_a).then_inc(cross_in, 16)
            sp.dma_start(CROSS_B, cross_b).then_inc(cross_in, 16)
            for i in range(4):
                sp.dma_start(W1T[:, 8 * i:8 * i + 8, :], w1t[:, 8 * i:8 * i + 8, :]).then_inc(w1_in[i], 16)
            sp.dma_start(NEAR, near_a).then_inc(near_in, 16)
            sp.dma_start(NEAR_B, near_b).then_inc(near_in, 16)
            for dst, src in ((b0s[:, :], b0), (b1s[:, :], b1), (bt1s[:, :], bt1), (bt2s[:, :], bt2),
                             (wt3s[:, :], wt3), (CTX[:, :], ctxt)):
                sp.dma_start(dst, src).then_inc(small_in, 16)
            sp.dma_start(W0Z[:, :, :], w0z).then_inc(w0z_in, 16)
            for c in range(NC):
                sp.wait_ge(b7_ev, use7["t2", c, NK - 1] + 1)
                if c:
                    sp.wait_ge(z0_mm, c)
                else:
                    sp.wait_ge(dt_mm, NDT)
                for q in range(4):
                    for quad in range(2):
                        for dst, r in ((GL, 0), (GG, F)):
                            sp.dma_start(
                                dst[32 * q:32 * q + 32, quad::2, :, :],
                                T2[64 * quad + r:64 * quad + r + F, :, :].rearrange("p (h m) b -> p h m b", h=2)[:, :, 8 * q:8 * q + 8, :],
                            ).then_inc(g_in, 16)
                if c == NC - 1:
                    sp.dma_start(WT1, wt1[0:2 * P, :].rearrange("(k p) n -> p k n", p=P)).then_inc(mlp_in, 16)
                    sp.dma_start(WT1C, wt1[2 * P:, :]).then_inc(mlp_in, 16)
                    sp.dma_start(WT2, wt2.rearrange("(k p) n -> p k n", p=P)).then_inc(mlp_in, 16)
            sp.wait_ge(y_ev, 1)
            sp.dma_start(out.rearrange("b o -> o b"), Y[:, :]).then_inc(out_done, 16)
            sp.wait_ge(out_done, 16)

        @block.gpsimd
        def _(pool):
            pool.memset(ident[:, :], 0.0).then_inc(id_zero, 1)
            pool.wait_ge(id_zero, 1)
            pool.affine_select(out=ident[:, :], in_=ident[:, :], compare_op=ALU.not_equal, fill=1.0, base=0,
                               pattern=[[-1, P]], channel_multiplier=1).then_inc(id_done, 1)
            pool.wait_ge(ids_in, 16)
            for c in range(NC):
                if c:
                    pool.wait_ge(s_red, 2 * c)
                for f in range(F):
                    if c and f % 8 == 0:
                        pool.wait_ge(gathered[f // 8], 128 * c)
                    if c and f % 4 == 0:
                        pool.wait_ge(x_mm, NG * (c - 1) + f // 4 + 1)
                    pool.indirect_dma_start(
                        out=XG[:, f, :], out_offset=None, in_=tables[f],
                        in_offset=bass.IndirectOffsetOnAxis(ap=idx[:, c, f:f + 1], axis=0),
                    ).then_inc(gathered[f // 8], 16)

        @block.vector
        def _(dve):
            v = nc.vector
            v.memset(XB[0:64, :, F:2 * F], 0.0).then_inc(zeroed, 1)
            v.memset(XB[64:128, :, 0:F], 0.0).then_inc(zeroed, 1)
            dve.wait_ge(cross_in, 32)
            v.tensor_tensor(CROSS, CROSS, CROSS_B, ALU.add).then_inc(cross_sum, 1)
            v.memset(PP[:, :, :, CL + 2 * NS:CX], 0.0).then_inc(zeroed, 1)
            v.memset(DL[:, :, :, 2 * NS:F], 0.0).then_inc(zeroed, 1)
            dve.wait_ge(near_in, 32)
            tiles, tiles_b = [x[:, 0:CL].rearrange("p (g n) -> p g n", g=2)[:, :, HF:] for x in (NEAR, NEAR_B)]
            v.tensor_tensor(tiles, tiles, tiles_b, ALU.add).then_inc(near_sum, 1)
            v.tensor_tensor(NEAR[:, CL:], NEAR[:, CL:], NEAR_B[:, CL:], ALU.add).then_inc(near_sum, 1)
            dve.wait_ge(small_in, 96)
            v.tensor_scalar_mul(b64[:, 0:1], b0s[:, :], float(DE)).then_inc(b_sum, 1)
            v.tensor_scalar_mul(b64[:, 1:2], b1s[:, :], float(DE)).then_inc(b_sum, 1)

            def move(half, second):
                if half == 0:
                    m0, col, mm, jj, ss = HF, 0, 1, NX + HF, (NX if second else HF)
                    base = F_AT
                else:
                    m0, col, mm, jj, ss = 0, P, HF, NX + 1, (NX if second else 1)
                    base = F_AT + HF * NX
                wrap = HF * ss
                for s in range(1 if second else 0, NS + 1):
                    if s == NS:
                        parts, at = ((0, NS),), D_AT + m0 * NN + CL + half * NS
                    else:
                        parts, at = ((0, HF - s), (HF - s, HF)), D_AT + m0 * NN + col + s * HF
                    for j0, j1 in parts:
                        if j1 == j0:
                            continue
                        d = in_main(at + j0, [[NN, HF], [1, j1 - j0]])
                        off = base + s * ss + j0 * jj - (wrap if j0 + s >= HF else 0)
                        last = v.tensor_tensor(d, d, in_main(off, [[mm, HF], [jj, j1 - j0]]), ALU.add)
                last.then_inc(moved, 1)

            def sum_rows(c):
                for q in range(NQ):
                    dve.wait_ge(gathered[q], 128 * (c + 1))
                if c:
                    dve.wait_ge(st_mm, c)
                v.tensor_reduce(S[:, :], XG[:, 0:F, :], AX.X, ALU.add).then_inc(s_red, 1)
                v.tensor_copy(XG[:, F, :], XG[:, 0, :]).then_inc(s_red, 1)

            for n, half in enumerate((1, 0)):
                dve.wait_ge(v_ev, F + HF * (n + 1))
                move(half, False)
                dve.wait_ge(moved, 2 * n + 1)
                move(half, True)
                if n == 0:
                    sum_rows(0)
            dve.wait_ge(moved, 4)
            v.tensor_copy(DL[:, :, :, 0:2 * NS],
                          D[:, :, CL:].rearrange("p (q m) r -> p m q r", q=4)).then_inc(left, 1)
            for n in range(9, NDT, 2):
                dve.wait_ge(dt_mm, n + 1)
                dst = DT[:, 2 * n:2 * n + 2, :, :] if n < 16 else DLT[:, 4 * (n - 16):4 * (n - 16) + 4, :]
                v.tensor_copy(dst.rearrange("p a b o -> p (a b o)") if n < 16 else dst.rearrange("p a o -> p (a o)"),
                              bank[4 + n % 2]).then_inc(dt_dve, 1)

            def repeat(c):
                dve.wait_ge(b7_ev, use7["x", c, NG - 1] + 1)
                xt = XT[:, c % 2].rearrange("p b (g m) -> p b g m", g=2)
                v.tensor_copy(xt[:, :, :, HF:XW], xt[:, :, :, 0:NS]).then_inc(xt_full, 1)
                dve.wait_ge(xt_full, c + 1)

            def spread(c):
                if c:
                    dve.wait_ge(t_mm, NK * c)
                for lo in (0, 64):
                    xt = XT[lo:lo + 64, c % 2].rearrange("p b (g m) -> p b g m", g=2)[:, :, :, 0:HF]
                    xb = XB[lo:lo + 64, :, lo // 2:lo // 2 + F].rearrange("p b (g m) -> p b g m", g=2)
                    v.tensor_copy(xb, xt).then_inc(xb_done, 1)

            def products(c, k):
                n = NK * c + k
                if n >= PPS:
                    dve.wait_ge(t_mm, n - PPS + 1)
                pp = PP[:, n % PPS]
                x0 = (c % 2) * xt_n + KB * k * 2 * XW
                for g in range(2):
                    at = x0 + g * XW
                    v.tensor_tensor(pp[:, :, g * P:(g + 1) * P].rearrange("p b (s j) -> p b s j", s=NS),
                                    in_main(at, [[2 * XW, KB], [0, NS], [1, HF]]),
                                    in_main(at, [[2 * XW, KB], [1, NS], [1, HF]]), ALU.mult)
                x = XT[:, c % 2, KB * k:KB * k + KB].rearrange("p b (g m) -> p b g m", g=2)
                v.tensor_copy(pp[:, :, CX:NP].rearrange("p b (g m) -> p b g m", g=2), x[:, :, :, 0:HF])
                v.tensor_tensor(pp[:, :, CL:CL + 2 * NS].rearrange("p b (g m) -> p b g m", g=2),
                                x[:, :, :, 0:NS], x[:, :, :, NS:HF], ALU.mult).then_inc(pp_ready, 1)

            repeat(0)
            products(0, 0)
            spread(0)
            for c in range(NC):
                for k in range(1, NK):
                    products(c, k)
                    if k == XK - 1 and c < NC - 1:
                        sum_rows(c + 1)
                if c < NC - 1:
                    repeat(c + 1)
                    products(c + 1, 0)
                    spread(c + 1)

            for k in (1, 3):
                dve.wait_ge(h1_mm, k + 1)
                v.tensor_scalar(H1[:, k, :], bank[k], bt1s[:, k:k + 1], 0.0, ALU.add, ALU.max).then_inc(h1_ev, 1)
            dve.wait_ge(h2_mm, 2)
            v.tensor_scalar(H2[:, 1, :], bank[5], bt2s[:, 1:2], 0.0, ALU.add, ALU.max).then_inc(h2_ev, 1)

        @block.scalar
        def _(act):
            a = nc.scalar

            def copy(dst, src):
                return a.activation(dst, src, ACT.Copy)

            for m in range(F):
                act.wait_ge(v_mm, m + 1)
                copy(FX[:, m, :], bank[m % 4][:, 0:NX]).then_inc(v_ev, 1)
            act.wait_ge(lin_mm, 1)
            copy(LS[:, :], bank[6][:, 0:F]).then_inc(lin_ev, 1)
            act.wait_ge(lin_mm, 2)
            copy(LT[:, :], bank[6][0:F, 0:H]).then_inc(lin_ev, 1)
            for m in range(F):
                act.wait_ge(v_mm, F + m + 1)
                copy(D[:, m, :], bank[m % 4][:, 0:NN]).then_inc(v_ev, 1)

            def dt_out(n):
                act.wait_ge(dt_mm, n + 1)
                dst = DT[:, 2 * n:2 * n + 2, :, :].rearrange("p a b o -> p (a b o)") if n < 16 else \
                    DLT[:, 4 * (n - 16):4 * (n - 16) + 4, :].rearrange("p a o -> p (a o)")
                copy(dst, bank[4 + n % 2]).then_inc(dt_act, 1)

            def x_out(c, g):
                act.wait_ge(x_mm, NG * c + g + 1)
                src = bank[7].rearrange("p (m b) -> p b m", m=4)
                xt = XT[:, c % 2]
                at = 4 * g + (g // 4) * NS
                copy(xt[0:64, :, at:at + 4], src[0:64, 0:BP, :])
                n = 4 if g % 4 < 3 else 3
                last = copy(xt[64:128, :, at + 1:at + 1 + n], src[64:128, BP:P, 0:n])
                if n == 3:
                    at = XW if g < 4 else 0
                    last = copy(xt[64:128, :, at:at + 1], src[64:128, BP:P, 3:4])
                last.then_inc(b7_ev, 1)

            for n in range(8):
                dt_out(n)
            for g in range(NG):
                x_out(0, g)
            for n in range(8, NDT, 2):
                dt_out(n)
            act.wait_ge(b_sum, 2)

            def moments_out(n):
                act.wait_ge(t_mm, n + 1)
                if n >= 2:
                    act.wait_ge(tr_mm, n - 1)
                src = psum[:, 2 * (n % 2):2 * (n % 2) + 2, :]
                copy(U[:, n % 2, :].rearrange("p (q n) -> p q n", q=2), src[:, :, 0:CL])
                copy(U2[:, n % 2, :].rearrange("p (q n) -> p q n", q=2), src[:, :, CL:NP]).then_inc(u_ev, 1)

            def transposed_out(c, k):
                n = NK * c + k
                act.wait_ge(tr_mm, n + 1)
                if k == 0 and c:
                    act.wait_ge(g_in, 256 * c)
                src = bank[4 + n % 2].rearrange("p (q t i n) -> p q t n i", q=2, t=2, i=2)
                for quad in range(2):
                    b = quad * (BP // 2) + 2 * k
                    last = copy(T[:, c % 2, :, :, b:b + 2], src[:, quad])
                last.then_inc(tr_ev, 1)
                copy(T2[:, :, 2 * k:2 * k + 2], bank[7][:, 0:P].rearrange("p (i n) -> p n i", i=2)).then_inc(b7_ev, 1)

            def z1_out(c):
                act.wait_ge(z1_mm, c + 1)
                a.activation(ZT[:, 1, P * c:P * c + P], bank[6][:, 0:P], ACT.Identity, bias=b64[:, 1:2]).then_inc(z1_ev, 1)

            def z0_out(c):
                act.wait_ge(z0_mm, c + 1)
                a.activation(ZT[:, 0, P * c:P * c + P], bank[7][:, 0:P], ACT.Identity, bias=b64[:, 0:1]).then_inc(b7_ev, 1)

            for c in range(NC):
                for k in range(NK):
                    moments_out(NK * c + k)
                    if k:
                        transposed_out(c, k - 1)
                    if k == 2:
                        act.wait_ge(st_mm, c + 1)
                        for h in range(2):
                            last = copy(ST[:, 64 * h:64 * h + 64].rearrange("p (q k i) -> p q k i", q=2, i=2),
                                        bank[7][0:F, 64 * h:64 * h + 64].rearrange("p (k q i) -> p q k i", q=2, i=2))
                        last.then_inc(b7_ev, 1)
                    if c < NC - 1 and XK <= k < XK + NG:
                        x_out(c + 1, k - XK)
                transposed_out(c, NK - 1)
                if c:
                    z1_out(c - 1)
                    z0_out(c - 1)
            z1_out(NC - 1)
            z0_out(NC - 1)

            for k in (0, 2):
                act.wait_ge(h1_mm, k + 1)
                a.activation(H1[:, k, :], bank[k], ACT.Relu, bias=bt1s[:, k:k + 1]).then_inc(h1_ev, 1)
            act.wait_ge(h2_mm, 1)
            a.activation(H2[:, 0, :], bank[4], ACT.Relu, bias=bt2s[:, 0:1]).then_inc(h2_ev, 1)
            act.wait_ge(y_mm, 1)
            copy(Y[:, :], bank[6][0:1, :]).then_inc(y_ev, 1)

        @block.tensor
        def _(pe):
            mm, transpose = nc.tensor.matmul, nc.tensor.transpose

            for n in range(2 * F):
                m = n % F
                if n == 0:
                    pe.wait_ge(cross_sum, 1)
                if n == F:
                    pe.wait_ge(near_sum, 2)
                if n < F and m % 8 == 0:
                    pe.wait_ge(w1_in[m // 8], 16)
                if n >= 4:
                    pe.wait_ge(v_ev, n - 3)
                cols, pairs = (NX, CROSS) if n < F else (NN, NEAR)
                mm(bank[m % 4][:, 0:cols], W1T[:, m, :], pairs, start=True, stop=True).then_inc(v_mm, 1)
                if n == F - 1:
                    pe.wait_ge(small_in, 96)
                    for i in range(F):
                        last = mm(bank[6][:, i:i + 1], W1T[:, i, :], b0s[:, :], start=True, stop=True)
                    last.then_inc(lin_mm, 1)
                    pe.wait_ge(lin_ev, 1)
                    pe.wait_ge(id_done, 1)
                    mm(bank[6][0:F, 0:H], LS[:, :], ident[:, :], start=True, stop=True).then_inc(lin_mm, 1)

            def coefficients(n):
                if n >= 2:
                    pe.wait_ge(*dt_engine(n - 2))
                for i in range(4):
                    src = D[:, 2 * n + i // 2, (i % 2) * P:(i % 2) * P + P] if n < 16 else \
                        DL[:, 4 * (n - 16) + i, :, :].rearrange("p q r -> p (q r)")
                    last = transpose(bank[4 + n % 2][:, i * P:(i + 1) * P], src, ident[:, :])
                last.then_inc(dt_mm, 1)

            def bank7(*use):
                if use7[use]:
                    pe.wait_ge(b7_ev, use7[use])

            def x_group(c, g):
                if g == 0:
                    pe.wait_ge(gathered[0], 128 * (c + 1))
                if g % 2 and g < 7:
                    pe.wait_ge(gathered[g // 2 + 1], 128 * (c + 1))
                if g == 7:
                    pe.wait_ge(s_red, 2 * c + 2)
                bank7("x", c, g)
                for i in range(4):
                    last = transpose(bank[7][:, i * P:(i + 1) * P],
                                     XG[:, 4 * g + i:4 * g + i + 2, :].rearrange("p f d -> p (f d)"), ident[:, :])
                last.then_inc(x_mm, 1)

            pe.wait_ge(moved, 2)
            for n in range(8):
                coefficients(n)
            for g in range(NG):
                x_group(0, g)
            pe.wait_ge(moved, 4)
            for n in range(8, 16):
                coefficients(n)
            pe.wait_ge(left, 1)
            pe.wait_ge(zeroed, 4)
            for n in range(16, NDT):
                coefficients(n)

            def moments(c, k):
                n = NK * c + k
                pe.wait_ge(pp_ready, n + 1)
                if k == 0:
                    pe.wait_ge(xb_done, 2 * c + 2)
                if n == 0:
                    pe.wait_ge(v_ev, 2 * F)
                if n >= 2:
                    pe.wait_ge(u_ev, n - 1)
                for i in range(KB):
                    last = mm(bank[2 * (n % 2) + i // 2][64 * (i % 2):64 * (i % 2) + 64, 0:NP],
                              XB[:, KB * k + i, :], PP[:, n % PPS, i, :], start=True, stop=True)
                last.then_inc(t_mm, 1)

            def turn(c, k):
                n = NK * c + k
                pe.wait_ge(u_ev, n + 1)
                if n >= 2:
                    pe.wait_ge(tr_ev, n - 1)
                else:
                    pe.wait_ge(*dt_engine(NDT - 2 + n % 2))
                for i in range(4):
                    transpose(bank[4 + n % 2][:, i * P:(i + 1) * P], U[:, n % 2, i * P:(i + 1) * P], ident[:, :])
                bank7("t2", c, k)
                transpose(bank[7][:, 0:P], U2[:, n % 2, :], ident[:, :]).then_inc(tr_mm, 1)

            def contract(c):
                pe.wait_ge(b7_ev, use7["s", c, 0] + 1)
                if c:
                    pe.wait_ge(z1_ev, c)
                mm(bank[6][:, 0:P], LT[:, :], ST[:, :], start=True, stop=False)
                z = bank[6][:, 0:P].rearrange("p (h b) -> p h b", h=2)
                pe.wait_ge(tr_ev, NK * (c + 1))
                for m in range(F):
                    for t in range(2):
                        mm(z, DT[:, m, t, :], T[:, c % 2, t].rearrange("p (h m) b -> p h m b", h=2)[:, :, m, :],
                           start=False, stop=False)
                        yield
                z = bank[6][:, 0:P].rearrange("p (a b) -> p a b", a=4)
                pe.wait_ge(g_in, 256 * (c + 1))
                for m in range(8):
                    last = mm(z, DLT[:, m, :], GL[:, :, m, :], start=False, stop=m == 7)
                    if m < 7:
                        yield
                last.then_inc(z1_mm, 1)
                yield

            def gram(c):
                bank7("z0", c, 0)
                if c == 0:
                    pe.wait_ge(w0z_in, 16)
                z = bank[7][:, 0:P].rearrange("p (a b) -> p a b", a=4)
                for m in range(8):
                    last = mm(z, W0Z[:, m, :], GG[:, :, m, :], start=m == 0, stop=m == 7)
                last.then_inc(z0_mm, 1)

            def s_rows(c):
                pe.wait_ge(s_red, 2 * c + 1)
                bank7("s", c, 0)
                mm(bank[7][0:F, 0:P], S[:, :], ident[:, :], start=True, stop=True).then_inc(st_mm, 1)

            for c in range(NC):
                last_chunk = contract(c - 1) if c else iter(())
                for k in range(NK):
                    moments(c, k)
                    next(last_chunk, None)
                    next(last_chunk, None)
                    if k:
                        turn(c, k - 1)
                    if k == 2:
                        s_rows(c)
                    next(last_chunk, None)
                    next(last_chunk, None)
                    if c < NC - 1 and XK <= k < XK + NG:
                        x_group(c + 1, k - XK)
                next(last_chunk, None)
                next(last_chunk, None)
                next(last_chunk, None)
                turn(c, NK - 1)
                for _ in last_chunk:
                    pass
                if c:
                    gram(c - 1)
            for _ in contract(NC - 1):
                pass
            gram(NC - 1)

            pe.wait_ge(mlp_in, 48)
            pe.wait_ge(z1_ev, NC)
            pe.wait_ge(b7_ev, use7["z0", NC - 1, 0] + 1)
            for k in range(4):
                cols = slice(k * P, (k + 1) * P)
                mm(bank[k], WT1[:, 0, cols], ZT[:, 0, :], start=True, stop=False)
                mm(bank[k], WT1[:, 1, cols], ZT[:, 1, :], start=False, stop=False)
                mm(bank[k], WT1C[:, cols], CTX[:, :], start=False, stop=True).then_inc(h1_mm, 1)
            pe.wait_ge(h1_ev, 4)
            for n in range(2):
                for k in range(4):
                    last = mm(bank[4 + n], WT2[:, k, n * P:(n + 1) * P], H1[:, k, :], start=k == 0, stop=k == 3)
                last.then_inc(h2_mm, 1)
            pe.wait_ge(h2_ev, 2)
            for k in range(2):
                last = mm(bank[6][0:1, :], wt3s[:, k:k + 1], H2[:, k, :], start=k == 0, stop=k == 1)
            last.then_inc(y_mm, 1)


def kernel(**inputs):
    import concourse.bacc as bacc
    from concourse.bass_utils import run_bass_kernel_spmd

    a = {n: np.asarray(x) for n, x in inputs.items()}
    w0 = a["L0_rec_W0"].reshape(H, F, F)
    i, j = [], []
    for shifts in (range(NS), range(NS, NS + 1)):
        for g in range(2):
            for s in shifts:
                for n in range(HF if s < NS else NS):
                    i.append(HF * g + n)
                    j.append(HF * g + (n + s) % HF)
    h, k, q, r = np.meshgrid(range(2), range(NK), range(2), range(2), indexing="ij")
    row_of = (h * BP + q * (BP // 2) + 2 * k + r).ravel()
    arrays = {
        "ids": a["ids"].reshape(NC, P, F)[:, row_of, :].transpose(1, 0, 2),
        **{f"tbl_{f}": a[f"tbl_{f}"] for f in range(F)},
        "near_a": w0[:, i, j], "near_b": w0[:, j, i],
        "cross_a": w0[:, :HF, HF:].reshape(H, NX), "cross_b": w0[:, HF:, :HF].transpose(0, 2, 1).reshape(H, NX),
        "w1t": a["L0_rec_W1"].reshape(H, F, H).transpose(2, 1, 0),
        "w0z": w0.reshape(H, F, 4, 8).transpose(2, 1, 3, 0).reshape(P, 8, H),
        "b0": a["L0_rec_b0"].reshape(H, 1), "b1": a["L0_rec_b1"].reshape(H, 1),
        "ctxt": a["dense_ctx"].T, "wt1": a["W_top1"], "bt1": a["b_top1"].reshape(4, P).T,
        "wt2": a["W_top2"], "bt2": a["b_top2"].reshape(2, P).T, "wt3": a["W_top3"].reshape(2, P).T,
    }
    arrays = {n: np.ascontiguousarray(x) for n, x in arrays.items()}
    nc = bacc.Bacc("TRN2", target_bir_lowering=False, num_devices=1)
    d = {n: nc.dram_tensor(f"in_{n}", x.shape, mybir.dt.from_np(x.dtype), kind="ExternalInput").ap()
         for n, x in arrays.items()}
    out = nc.dram_tensor("out", (B, 1), mybir.dt.float32, kind="ExternalOutput").ap()
    build(nc, d["ids"], [d[f"tbl_{f}"] for f in range(F)], d["near_a"], d["near_b"], d["cross_a"], d["cross_b"],
          d["w1t"], d["w0z"], d["b0"], d["b1"], d["ctxt"], d["wt1"], d["bt1"], d["wt2"], d["bt2"], d["wt3"], out)
    r = run_bass_kernel_spmd(nc, [{f"in_{n}": x for n, x in arrays.items()}], core_ids=[0])
    return r.results[0]["out"]
```

```python
from contextlib import ExitStack

import numpy as np

import concourse.bass as bass
from concourse import mybir

B, F, DE, H = 512, 32, 64, 128
P = 128
NC = B // P
HF = F // 2
NS = HF // 2
NN = 2 * (NS * HF + NS)
NX = HF * HF
BP = P // 2
KB = 4
NK = BP // KB
CL = 2 * P
CX = CL + F
NP = CX + F
XW = HF + NS
PPS = 3
F1, F2 = 512, 256
DC = 16
NQ = 4
NG = 8
XK = 7
NDT = F // 2 + 2


def bank_uses():
    pair, seven = [("x", 0, g) for g in range(NG)], []
    for c in range(NC):
        for k in range(NK):
            d = [("d", 0, n) for n in range(3 * k, 3 * k + 3)] if c == 0 and 3 * k < NDT else []
            pair += d[:1]
            if k:
                pair.append(("t", c, k - 1))
                seven.append(("t2", c, k - 1))
            pair += d[1:]
            if k == 2:
                seven.append(("s", c, 0))
            if c < NC - 1 and XK <= k < XK + NG:
                pair.append(("x", c + 1, k - XK))
        pair.append(("t", c, NK - 1))
        seven.append(("t2", c, NK - 1))
        if c:
            seven.append(("z0", c - 1, 0))
    seven.append(("z0", NC - 1, 0))
    return pair, {u: n for n, u in enumerate(seven)}


def build(nc, ids, tables, near_a, near_b, cross_a, cross_b, w1t, w0z, b0, b1, ctxt, wt1, bt1, wt2, bt2, wt3, out):
    f32, i32 = mybir.dt.float32, mybir.dt.int32
    ALU, ACT = mybir.AluOpType, mybir.ActivationFunctionType
    AX = mybir.AxisListType

    with ExitStack() as ctx:
        def sb(name, shape, dt=f32):
            return ctx.enter_context(nc.sbuf_tensor(name, shape, dt))

        def sem(name):
            return ctx.enter_context(nc.semaphore(name))

        xt_n, t_n, t2_n = BP * 2 * XW, 2 * F * P, 2 * F * F
        T_AT = 2 * xt_n
        T2_AT = T_AT + 2 * t_n
        MAIN_N = T2_AT + 2 * t2_n
        F_AT, W1_AT = T_AT + t_n, T2_AT
        D_AT = F_AT - F * NN
        assert F_AT + F * NX <= T2_AT and W1_AT + F * H <= MAIN_N and D_AT >= xt_n
        main = sb("main", [P, MAIN_N])
        XT = main[:, 0:T_AT].rearrange("p (c b m) -> p c b m", c=2, m=2 * XW)
        T = main[:, T_AT:T2_AT].rearrange("p (c t n b) -> p c t n b", c=2, t=2, b=BP)
        T2 = main[:, T2_AT:MAIN_N].rearrange("p (c n b) -> p c n b", c=2, b=BP // 2)
        FX = main[:, F_AT:F_AT + F * NX].rearrange("p (m n) -> p m n", m=F)
        D = main[:, D_AT:F_AT].rearrange("p (m n) -> p m n", m=F)
        W1T = main[:, W1_AT:W1_AT + F * H].rearrange("p (m o) -> p m o", m=F)
        H2 = main[:, 0:2 * B].rearrange("p (k b) -> p k b", k=2)
        wt = T_AT + t_n
        WT1 = main[:, wt:wt + 2 * F1].rearrange("p (k n) -> p k n", k=2)
        WT1C = main[0:DC, wt + 2 * F1:wt + 3 * F1]
        WT2 = main[:, wt + 3 * F1:wt + 3 * F1 + 4 * F2].rearrange("p (k n) -> p k n", k=4)

        def in_main(at, dims):
            return bass.AP(main[:, 0:1].tensor, at, [[MAIN_N, P]] + dims)

        XB = sb("XB", [P, BP, 2 * F])
        PP = sb("PP", [P, PPS, KB, NP])
        U = sb("U", [P, 2, 2 * CL])
        U2 = sb("U2", [P, 2, 2 * 2 * F])
        DT = sb("DT", [P, F, 2, H])
        DLT = sb("DLT", [P, 8, H])
        GL = sb("GL", [P, 4, 8, F])
        GG = sb("GG", [P, 4, 8, F])
        W0Z = sb("W0Z", [P, 8, H])
        ZT = sb("ZT", [P, 2, B])
        XG = sb("XG", [P, F + 1, DE])
        H1 = XG[:, 0:F, :].rearrange("p f d -> p (f d)").rearrange("p (k b) -> p k b", k=4)
        DL = GL[:, :, :, :].rearrange("p a m b -> p (a m b)").rearrange("p (m q r) -> p m q r", m=8, q=4)
        gg = GG[:, :, :, :].rearrange("p a m b -> p (a m b)")
        NEAR, NEAR_B = gg[:, 0:NN], gg[:, NN:2 * NN]
        zt = ZT[:, :, :].rearrange("p z b -> p (z b)")
        CROSS, CROSS_B = zt[:, 0:NX], zt[:, NX:2 * NX]
        CTX = sb("CTX", [DC, B])
        Y = U[0:1, 0, :]
        ident = sb("ident", [P, P])
        idx = sb("idx", [P, NC, F], i32)
        S = sb("S", [P, F])
        ST = sb("ST", [F, P])
        LS = sb("LS", [P, F])
        LT = sb("LT", [F, H])
        b0s, b1s = sb("b0s", [P, 1]), sb("b1s", [P, 1])
        b64 = sb("b64", [P, 2])
        bt1s, bt2s, wt3s = sb("bt1s", [P, 4]), sb("bt2s", [P, 2]), sb("wt3s", [P, 2])
        psum = ctx.enter_context(nc.psum_tensor("psum", [P, 8, 512], f32))
        bank = [psum[:, i, :] for i in range(8)]

        ids_in, cross_in, near_in, small_in = sem("ids_in"), sem("cross_in"), sem("near_in"), sem("small_in")
        w1_in = [sem(f"w1_in{i}") for i in range(4)]
        w0z_in, mlp_in = sem("w0z_in"), sem("mlp_in")
        id_zero, id_done = sem("id_zero"), sem("id_done")
        gathered = [sem(f"gathered{i}") for i in range(NQ)]
        zeroed = sem("zeroed")
        cross_sum, near_sum, b_sum = sem("cross_sum"), sem("near_sum"), sem("b_sum")
        v_mm, v_ev = sem("v_mm"), sem("v_ev")
        moved, left = sem("moved"), sem("left")
        dt_mm = sem("dt_mm")
        pair_act, pair_dve = sem("pair_act"), sem("pair_dve")
        lin_mm, lin_ev = sem("lin_mm"), sem("lin_ev")
        x_mm, st_mm, st_ev = sem("x_mm"), sem("st_mm"), sem("st_ev")
        b7_ev = sem("b7_ev")
        xt_full, xb_done, s_red = sem("xt_full"), sem("xb_done"), sem("s_red")
        pp_ready = sem("pp_ready")
        t_mm, u_ev = sem("t_mm"), sem("u_ev")
        tr_mm = sem("tr_mm")
        g_in = sem("g_in")
        z1_mm, z1_ev, z0_mm, z0_ev = sem("z1_mm"), sem("z1_ev"), sem("z0_mm"), sem("z0_ev")
        h1_mm, h1_ev, h2_mm, h2_ev = sem("h1_mm"), sem("h1_ev"), sem("h2_mm"), sem("h2_ev")
        y_mm, y_ev, out_done = sem("y_mm"), sem("y_ev"), sem("out_done")

        pair_uses, use7 = bank_uses()
        pair_bank, pair_out, counts = {}, {}, {pair_act: 0, pair_dve: 0}
        for i, use in enumerate(pair_uses):
            by = pair_dve if use[0] == "d" and use[2] % 3 != 1 else pair_act
            counts[by] += 1
            pair_bank[use] = 4 + i % 2
            pair_out[use] = by, counts[by]
        pair_before = dict(zip(pair_uses[2:], pair_uses))

        def coefficient_slot(n):
            if n < F // 2:
                return DT[:, 2 * n:2 * n + 2, :, :].rearrange("p a b o -> p (a b o)")
            n -= F // 2
            return DLT[:, 4 * n:4 * n + 4, :].rearrange("p a o -> p (a o)")

        block = ctx.enter_context(nc.Block())

        @block.sync
        def _(sp):
            sp.dma_start(idx[:, :, :], ids).then_inc(ids_in, 16)
            sp.dma_start(CROSS, cross_a).then_inc(cross_in, 16)
            sp.dma_start(CROSS_B, cross_b).then_inc(cross_in, 16)
            for i in range(4):
                sp.dma_start(W1T[:, 8 * i:8 * i + 8, :], w1t[:, 8 * i:8 * i + 8, :]).then_inc(w1_in[i], 16)
            sp.dma_start(W0Z[:, :, :], w0z).then_inc(w0z_in, 16)
            for c in range(NC):
                sp.wait_ge(b7_ev, use7["t2", c, NK - 1] + 1)
                if c:
                    sp.wait_ge(z0_mm, c)
                else:
                    sp.wait_ge(dt_mm, NDT)
                for q in range(4):
                    for quad in range(2):
                        for dst, r in ((GL, 0), (GG, F)):
                            sp.dma_start(
                                dst[32 * q:32 * q + 32, quad::2, :, :],
                                T2[64 * quad + r:64 * quad + r + F, c % 2].rearrange("p (h m) b -> p h m b", h=2)[:, :, 8 * q:8 * q + 8, :],
                            ).then_inc(g_in, 16)
                if c == NC - 1:
                    sp.dma_start(WT1, wt1[0:2 * P, :].rearrange("(k p) n -> p k n", p=P)).then_inc(mlp_in, 16)
                    sp.dma_start(WT1C, wt1[2 * P:, :]).then_inc(mlp_in, 16)
                    sp.dma_start(WT2, wt2.rearrange("(k p) n -> p k n", p=P)).then_inc(mlp_in, 16)
            sp.wait_ge(y_ev, 1)
            sp.dma_start(out.rearrange("b o -> o b"), Y[:, :]).then_inc(out_done, 16)
            sp.wait_ge(out_done, 16)

        @block.gpsimd
        def _(pool):
            pool.memset(ident[:, :], 0.0).then_inc(id_zero, 1)
            pool.wait_ge(id_zero, 1)
            pool.affine_select(out=ident[:, :], in_=ident[:, :], compare_op=ALU.not_equal, fill=1.0, base=0,
                               pattern=[[-1, P]], channel_multiplier=1).then_inc(id_done, 1)
            pool.wait_ge(ids_in, 16)
            for c in range(NC):
                if c:
                    pool.wait_ge(s_red, 2 * c)
                for f in range(F):
                    if c and f % 8 == 0:
                        pool.wait_ge(gathered[f // 8], 128 * c)
                    if c and f % 4 == 0:
                        pool.wait_ge(x_mm, NG * (c - 1) + f // 4 + 1)
                    pool.indirect_dma_start(
                        out=XG[:, f, :], out_offset=None, in_=tables[f],
                        in_offset=bass.IndirectOffsetOnAxis(ap=idx[:, c, f:f + 1], axis=0),
                    ).then_inc(gathered[f // 8], 16)

        @block.vector
        def _(dve):
            v = nc.vector
            v.memset(XB[0:64, :, F:2 * F], 0.0).then_inc(zeroed, 1)
            v.memset(XB[64:128, :, 0:F], 0.0).then_inc(zeroed, 1)
            dve.wait_ge(cross_in, 32)
            v.tensor_tensor(CROSS, CROSS, CROSS_B, ALU.add).then_inc(cross_sum, 1)
            v.memset(PP[:, :, :, CL + 2 * NS:CX], 0.0).then_inc(zeroed, 1)
            v.memset(DL[:, :, :, 2 * NS:F], 0.0).then_inc(zeroed, 1)
            dve.wait_ge(near_in, 32)
            tiles, tiles_b = [x[:, 0:CL].rearrange("p (g n) -> p g n", g=2)[:, :, HF:] for x in (NEAR, NEAR_B)]
            v.tensor_tensor(tiles, tiles, tiles_b, ALU.add).then_inc(near_sum, 1)
            v.tensor_tensor(NEAR[:, CL:], NEAR[:, CL:], NEAR_B[:, CL:], ALU.add).then_inc(near_sum, 1)
            dve.wait_ge(small_in, 96)
            v.tensor_scalar_mul(b64[:, 0:1], b0s[:, :], float(DE)).then_inc(b_sum, 1)
            v.tensor_scalar_mul(b64[:, 1:2], b1s[:, :], float(DE)).then_inc(b_sum, 1)

            def move(half, second):
                if half == 0:
                    m0, col, mm, jj, ss = HF, 0, 1, NX + HF, (NX if second else HF)
                    base = F_AT
                else:
                    m0, col, mm, jj, ss = 0, P, HF, NX + 1, (NX if second else 1)
                    base = F_AT + HF * NX
                wrap = HF * ss
                for s in range(1 if second else 0, NS + 1):
                    if s == NS:
                        parts, at = ((0, NS),), D_AT + m0 * NN + CL + half * NS
                    else:
                        parts, at = ((0, HF - s), (HF - s, HF)), D_AT + m0 * NN + col + s * HF
                    for j0, j1 in parts:
                        if j1 == j0:
                            continue
                        d = in_main(at + j0, [[NN, HF], [1, j1 - j0]])
                        off = base + s * ss + j0 * jj - (wrap if j0 + s >= HF else 0)
                        last = v.tensor_tensor(d, d, in_main(off, [[mm, HF], [jj, j1 - j0]]), ALU.add)
                last.then_inc(moved, 1)

            def sum_rows(c):
                for q in range(NQ):
                    dve.wait_ge(gathered[q], 128 * (c + 1))
                if c:
                    dve.wait_ge(st_mm, c)
                v.tensor_reduce(S[:, :], XG[:, 0:F, :], AX.X, ALU.add).then_inc(s_red, 1)
                v.tensor_copy(XG[:, F, :], XG[:, 0, :]).then_inc(s_red, 1)

            for n, half in enumerate((1, 0)):
                dve.wait_ge(v_ev, F + HF * (n + 1))
                move(half, False)
                dve.wait_ge(moved, 2 * n + 1)
                move(half, True)
                if n == 0:
                    sum_rows(0)
            dve.wait_ge(moved, 4)
            v.tensor_copy(DL[:, :, :, 0:2 * NS],
                          D[:, :, CL:].rearrange("p (q m) r -> p m q r", q=4)).then_inc(left, 1)

            def repeat(c):
                dve.wait_ge(*pair_out["x", c, NG - 1])
                xt = XT[:, c % 2].rearrange("p b (g m) -> p b g m", g=2)
                v.tensor_copy(xt[:, :, :, HF:XW], xt[:, :, :, 0:NS]).then_inc(xt_full, 1)
                dve.wait_ge(xt_full, c + 1)

            def spread(c):
                if c:
                    dve.wait_ge(t_mm, NK * c)
                for lo in (0, 64):
                    xt = XT[lo:lo + 64, c % 2].rearrange("p b (g m) -> p b g m", g=2)[:, :, :, 0:HF]
                    xb = XB[lo:lo + 64, :, lo // 2:lo // 2 + F].rearrange("p b (g m) -> p b g m", g=2)
                    v.tensor_copy(xb, xt).then_inc(xb_done, 1)

            def products(c, k):
                n = NK * c + k
                if n >= PPS:
                    dve.wait_ge(t_mm, n - PPS + 1)
                pp = PP[:, n % PPS]
                x0 = (c % 2) * xt_n + KB * k * 2 * XW
                for g in range(2):
                    at = x0 + g * XW
                    v.tensor_tensor(pp[:, :, g * P:(g + 1) * P].rearrange("p b (s j) -> p b s j", s=NS),
                                    in_main(at, [[2 * XW, KB], [0, NS], [1, HF]]),
                                    in_main(at, [[2 * XW, KB], [1, NS], [1, HF]]), ALU.mult)
                x = XT[:, c % 2, KB * k:KB * k + KB].rearrange("p b (g m) -> p b g m", g=2)
                v.tensor_copy(pp[:, :, CX:NP].rearrange("p b (g m) -> p b g m", g=2), x[:, :, :, 0:HF])
                v.tensor_tensor(pp[:, :, CL:CL + 2 * NS].rearrange("p b (g m) -> p b g m", g=2),
                                x[:, :, :, 0:NS], x[:, :, :, NS:HF], ALU.mult).then_inc(pp_ready, 1)

            repeat(0)
            products(0, 0)
            spread(0)
            for c in range(NC):
                for k in range(1, NK):
                    products(c, k)
                    if c == 0:
                        for n in range(3 * k - 3, min(3 * k, NDT)):
                            if pair_out["d", 0, n][0] is pair_dve:
                                dve.wait_ge(dt_mm, n + 1)
                                v.tensor_copy(coefficient_slot(n), bank[pair_bank["d", 0, n]]).then_inc(pair_dve, 1)
                    if k == XK + NG - 2 and c < NC - 1:
                        sum_rows(c + 1)
                if c < NC - 1:
                    repeat(c + 1)
                    products(c + 1, 0)
                    spread(c + 1)

            for k in (1, 3):
                dve.wait_ge(h1_mm, k + 1)
                v.tensor_scalar(H1[:, k, :], bank[k], bt1s[:, k:k + 1], 0.0, ALU.add, ALU.max).then_inc(h1_ev, 1)
            dve.wait_ge(h2_mm, 2)
            v.tensor_scalar(H2[:, 1, :], bank[5], bt2s[:, 1:2], 0.0, ALU.add, ALU.max).then_inc(h2_ev, 1)

        @block.scalar
        def _(act):
            a = nc.scalar

            def copy(dst, src):
                return a.activation(dst, src, ACT.Copy)

            for dst, src in ((NEAR, near_a), (NEAR_B, near_b)):
                act.dma_start(dst, src).then_inc(near_in, 16)
            for dst, src in ((b0s[:, :], b0), (b1s[:, :], b1), (bt1s[:, :], bt1), (bt2s[:, :], bt2),
                             (wt3s[:, :], wt3), (CTX[:, :], ctxt)):
                act.dma_start(dst, src).then_inc(small_in, 16)
            for m in range(F):
                act.wait_ge(v_mm, m + 1)
                copy(FX[:, m, :], bank[m % 4][:, 0:NX]).then_inc(v_ev, 1)
            act.wait_ge(lin_mm, 1)
            copy(LS[:, :], bank[6][:, 0:F]).then_inc(lin_ev, 1)
            act.wait_ge(lin_mm, 2)
            copy(LT[:, :], bank[6][0:F, 0:H]).then_inc(lin_ev, 1)
            for m in range(F):
                act.wait_ge(v_mm, F + m + 1)
                copy(D[:, m, :], bank[m % 4][:, 0:NN]).then_inc(v_ev, 1)

            def dt_out(n):
                if pair_out["d", 0, n][0] is pair_act:
                    act.wait_ge(dt_mm, n + 1)
                    copy(coefficient_slot(n), bank[pair_bank["d", 0, n]]).then_inc(pair_act, 1)

            def x_out(c, g):
                act.wait_ge(x_mm, NG * c + g + 1)
                src = bank[pair_bank["x", c, g]].rearrange("p (m b) -> p b m", m=4)
                xt = XT[:, c % 2]
                at = 4 * g + (g // 4) * NS
                copy(xt[0:64, :, at:at + 4], src[0:64, 0:BP, :])
                n = 4 if g % 4 < 3 else 3
                last = copy(xt[64:128, :, at + 1:at + 1 + n], src[64:128, BP:P, 0:n])
                if n == 3:
                    at = XW if g < 4 else 0
                    last = copy(xt[64:128, :, at:at + 1], src[64:128, BP:P, 3:4])
                last.then_inc(pair_act, 1)

            for g in range(NG):
                x_out(0, g)
            act.wait_ge(b_sum, 2)

            def moments_out(n):
                act.wait_ge(t_mm, n + 1)
                if n >= 2:
                    act.wait_ge(tr_mm, n - 1)
                src = psum[:, 2 * (n % 2):2 * (n % 2) + 2, :]
                copy(U[:, n % 2, :].rearrange("p (q n) -> p q n", q=2), src[:, :, 0:CL])
                copy(U2[:, n % 2, :].rearrange("p (q n) -> p q n", q=2), src[:, :, CL:NP]).then_inc(u_ev, 1)

            def transposed_out(c, k):
                n = NK * c + k
                act.wait_ge(tr_mm, n + 1)
                if k == 0 and c == 0:
                    act.wait_ge(moved, 4)
                if k == 0 and c >= 2:
                    act.wait_ge(g_in, 256 * (c - 1))
                src = bank[pair_bank["t", c, k]].rearrange("p (q t i n) -> p q t n i", q=2, t=2, i=2)
                for quad in range(2):
                    b = quad * (BP // 2) + 2 * k
                    last = copy(T[:, (c + 1) % 2, :, :, b:b + 2], src[:, quad])
                last.then_inc(pair_act, 1)
                copy(T2[:, c % 2, :, 2 * k:2 * k + 2], bank[7][:, 0:P].rearrange("p (i n) -> p n i", i=2)).then_inc(b7_ev, 1)

            def z1_out(c):
                act.wait_ge(z1_mm, c + 1)
                a.activation(ZT[:, 1, P * c:P * c + P], bank[6][:, 0:P], ACT.Identity, bias=b64[:, 1:2]).then_inc(z1_ev, 1)

            def z0_out(c):
                act.wait_ge(z0_mm, c + 1)
                a.activation(ZT[:, 0, P * c:P * c + P], bank[7][:, 0:P], ACT.Identity, bias=b64[:, 0:1]).then_inc(b7_ev, 1)

            for c in range(NC):
                for k in range(NK):
                    moments_out(NK * c + k)
                    if k:
                        transposed_out(c, k - 1)
                    if c == 0 and 3 * k < NDT:
                        dt_out(3 * k + 1)
                    if k == 2:
                        act.wait_ge(st_mm, c + 1)
                        for h in range(2):
                            last = copy(ST[:, 64 * h:64 * h + 64].rearrange("p (q k i) -> p q k i", q=2, i=2),
                                        bank[7][0:F, 64 * h:64 * h + 64].rearrange("p (k q i) -> p q k i", q=2, i=2))
                        last.then_inc(b7_ev, 1)
                    if c < NC - 1 and XK <= k < XK + NG:
                        x_out(c + 1, k - XK)
                transposed_out(c, NK - 1)
                if c:
                    z1_out(c - 1)
                    z0_out(c - 1)
            z1_out(NC - 1)
            z0_out(NC - 1)

            for k in (0, 2):
                act.wait_ge(h1_mm, k + 1)
                a.activation(H1[:, k, :], bank[k], ACT.Relu, bias=bt1s[:, k:k + 1]).then_inc(h1_ev, 1)
            act.wait_ge(h2_mm, 1)
            a.activation(H2[:, 0, :], bank[4], ACT.Relu, bias=bt2s[:, 0:1]).then_inc(h2_ev, 1)
            act.wait_ge(y_mm, 1)
            copy(Y[:, :], bank[6][0:1, :]).then_inc(y_ev, 1)

        @block.tensor
        def _(pe):
            mm, transpose = nc.tensor.matmul, nc.tensor.transpose

            for n in range(2 * F):
                m = n % F
                if n == 0:
                    pe.wait_ge(cross_sum, 1)
                if n == F:
                    pe.wait_ge(near_sum, 2)
                if n < F and m % 8 == 0:
                    pe.wait_ge(w1_in[m // 8], 16)
                if n >= 4:
                    pe.wait_ge(v_ev, n - 3)
                cols, pairs = (NX, CROSS) if n < F else (NN, NEAR)
                mm(bank[m % 4][:, 0:cols], W1T[:, m, :], pairs, start=True, stop=True).then_inc(v_mm, 1)
                if n == F - 1:
                    pe.wait_ge(small_in, 96)
                    for i in range(F):
                        last = mm(bank[6][:, i:i + 1], W1T[:, i, :], b0s[:, :], start=True, stop=True)
                    last.then_inc(lin_mm, 1)
                    pe.wait_ge(lin_ev, 1)
                    pe.wait_ge(id_done, 1)
                    mm(bank[6][0:F, 0:H], LS[:, :], ident[:, :], start=True, stop=True).then_inc(lin_mm, 1)

            def coefficients(n):
                pe.wait_ge(*pair_out[pair_before["d", 0, n]])
                to = bank[pair_bank["d", 0, n]]
                for i in range(4):
                    src = D[:, 2 * n + i // 2, (i % 2) * P:(i % 2) * P + P] if n < 16 else \
                        DL[:, 4 * (n - 16) + i, :, :].rearrange("p q r -> p (q r)")
                    last = transpose(to[:, i * P:(i + 1) * P], src, ident[:, :])
                last.then_inc(dt_mm, 1)

            def bank7(*use):
                if use7[use]:
                    pe.wait_ge(b7_ev, use7[use])

            def x_group(c, g):
                if g == 0:
                    pe.wait_ge(gathered[0], 128 * (c + 1))
                if g % 2 and g < 7:
                    pe.wait_ge(gathered[g // 2 + 1], 128 * (c + 1))
                if g == 7:
                    pe.wait_ge(s_red, 2 * c + 2)
                if (use := ("x", c, g)) in pair_before:
                    pe.wait_ge(*pair_out[pair_before[use]])
                for i in range(4):
                    last = transpose(bank[pair_bank[use]][:, i * P:(i + 1) * P],
                                     XG[:, 4 * g + i:4 * g + i + 2, :].rearrange("p f d -> p (f d)"), ident[:, :])
                last.then_inc(x_mm, 1)

            for g in range(NG):
                x_group(0, g)
            pe.wait_ge(left, 1)
            pe.wait_ge(zeroed, 4)

            def moments(c, k):
                n = NK * c + k
                pe.wait_ge(pp_ready, n + 1)
                if k == 0:
                    pe.wait_ge(xb_done, 2 * c + 2)
                if n == 0:
                    pe.wait_ge(v_ev, 2 * F)
                if n >= 2:
                    pe.wait_ge(u_ev, n - 1)
                for i in range(KB):
                    last = mm(bank[2 * (n % 2) + i // 2][64 * (i % 2):64 * (i % 2) + 64, 0:NP],
                              XB[:, KB * k + i, :], PP[:, n % PPS, i, :], start=True, stop=True)
                last.then_inc(t_mm, 1)

            def turn(c, k):
                n = NK * c + k
                pe.wait_ge(u_ev, n + 1)
                use = ("t", c, k)
                pe.wait_ge(*pair_out[pair_before[use]])
                for i in range(4):
                    transpose(bank[pair_bank[use]][:, i * P:(i + 1) * P], U[:, n % 2, i * P:(i + 1) * P], ident[:, :])
                bank7("t2", c, k)
                transpose(bank[7][:, 0:P], U2[:, n % 2, :], ident[:, :]).then_inc(tr_mm, 1)

            def contract(c):
                pe.wait_ge(b7_ev, use7["s", c, 0] + 1)
                if c:
                    pe.wait_ge(z1_ev, c)
                mm(bank[6][:, 0:P], LT[:, :], ST[:, :], start=True, stop=False)
                z = bank[6][:, 0:P].rearrange("p (h b) -> p h b", h=2)
                pe.wait_ge(*pair_out["t", c, NK - 1])
                for m in range(F):
                    for t in range(2):
                        mm(z, DT[:, m, t, :], T[:, (c + 1) % 2, t].rearrange("p (h m) b -> p h m b", h=2)[:, :, m, :],
                           start=False, stop=False)
                        yield
                z = bank[6][:, 0:P].rearrange("p (a b) -> p a b", a=4)
                pe.wait_ge(g_in, 256 * (c + 1))
                for m in range(8):
                    last = mm(z, DLT[:, m, :], GL[:, :, m, :], start=False, stop=m == 7)
                    if m < 7:
                        yield
                last.then_inc(z1_mm, 1)
                yield

            def gram(c):
                bank7("z0", c, 0)
                if c == 0:
                    pe.wait_ge(w0z_in, 16)
                z = bank[7][:, 0:P].rearrange("p (a b) -> p a b", a=4)
                for m in range(8):
                    last = mm(z, W0Z[:, m, :], GG[:, :, m, :], start=m == 0, stop=m == 7)
                last.then_inc(z0_mm, 1)

            def s_rows(c):
                pe.wait_ge(s_red, 2 * c + 1)
                bank7("s", c, 0)
                mm(bank[7][0:F, 0:P], S[:, :], ident[:, :], start=True, stop=True).then_inc(st_mm, 1)

            for c in range(NC):
                last_chunk = contract(c - 1) if c else iter(())
                for k in range(NK):
                    moments(c, k)
                    next(last_chunk, None)
                    next(last_chunk, None)
                    mine = range(3 * k, 3 * k + 3) if c == 0 and 3 * k < NDT else ()
                    for n in mine[:1]:
                        coefficients(n)
                    if k:
                        turn(c, k - 1)
                    for n in mine[1:]:
                        coefficients(n)
                    if k == 2:
                        s_rows(c)
                    next(last_chunk, None)
                    next(last_chunk, None)
                    if c < NC - 1 and XK <= k < XK + NG:
                        x_group(c + 1, k - XK)
                next(last_chunk, None)
                next(last_chunk, None)
                next(last_chunk, None)
                turn(c, NK - 1)
                for _ in last_chunk:
                    pass
                if c:
                    gram(c - 1)
            for _ in contract(NC - 1):
                pass
            gram(NC - 1)

            pe.wait_ge(mlp_in, 48)
            pe.wait_ge(z1_ev, NC)
            pe.wait_ge(b7_ev, use7["z0", NC - 1, 0] + 1)
            for k in range(4):
                cols = slice(k * P, (k + 1) * P)
                mm(bank[k], WT1[:, 0, cols], ZT[:, 0, :], start=True, stop=False)
                mm(bank[k], WT1[:, 1, cols], ZT[:, 1, :], start=False, stop=False)
                mm(bank[k], WT1C[:, cols], CTX[:, :], start=False, stop=True).then_inc(h1_mm, 1)
            pe.wait_ge(h1_ev, 4)
            for n in range(2):
                for k in range(4):
                    last = mm(bank[4 + n], WT2[:, k, n * P:(n + 1) * P], H1[:, k, :], start=k == 0, stop=k == 3)
                last.then_inc(h2_mm, 1)
            pe.wait_ge(h2_ev, 2)
            for k in range(2):
                last = mm(bank[6][0:1, :], wt3s[:, k:k + 1], H2[:, k, :], start=k == 0, stop=k == 1)
            last.then_inc(y_mm, 1)


def kernel(**inputs):
    import concourse.bacc as bacc
    from concourse.bass_utils import run_bass_kernel_spmd

    a = {n: np.asarray(x) for n, x in inputs.items()}
    w0 = a["L0_rec_W0"].reshape(H, F, F)
    i, j = [], []
    for shifts in (range(NS), range(NS, NS + 1)):
        for g in range(2):
            for s in shifts:
                for n in range(HF if s < NS else NS):
                    i.append(HF * g + n)
                    j.append(HF * g + (n + s) % HF)
    h, k, q, r = np.meshgrid(range(2), range(NK), range(2), range(2), indexing="ij")
    row_of = (h * BP + q * (BP // 2) + 2 * k + r).ravel()
    arrays = {
        "ids": a["ids"].reshape(NC, P, F)[:, row_of, :].transpose(1, 0, 2),
        **{f"tbl_{f}": a[f"tbl_{f}"] for f in range(F)},
        "near_a": w0[:, i, j], "near_b": w0[:, j, i],
        "cross_a": w0[:, :HF, HF:].reshape(H, NX), "cross_b": w0[:, HF:, :HF].transpose(0, 2, 1).reshape(H, NX),
        "w1t": a["L0_rec_W1"].reshape(H, F, H).transpose(2, 1, 0),
        "w0z": w0.reshape(H, F, 4, 8).transpose(2, 1, 3, 0).reshape(P, 8, H),
        "b0": a["L0_rec_b0"].reshape(H, 1), "b1": a["L0_rec_b1"].reshape(H, 1),
        "ctxt": a["dense_ctx"].T, "wt1": a["W_top1"], "bt1": a["b_top1"].reshape(4, P).T,
        "wt2": a["W_top2"], "bt2": a["b_top2"].reshape(2, P).T, "wt3": a["W_top3"].reshape(2, P).T,
    }
    arrays = {n: np.ascontiguousarray(x) for n, x in arrays.items()}
    nc = bacc.Bacc("TRN2", target_bir_lowering=False, num_devices=1)
    d = {n: nc.dram_tensor(f"in_{n}", x.shape, mybir.dt.from_np(x.dtype), kind="ExternalInput").ap()
         for n, x in arrays.items()}
    out = nc.dram_tensor("out", (B, 1), mybir.dt.float32, kind="ExternalOutput").ap()
    build(nc, d["ids"], [d[f"tbl_{f}"] for f in range(F)], d["near_a"], d["near_b"], d["cross_a"], d["cross_b"],
          d["w1t"], d["w0z"], d["b0"], d["b1"], d["ctxt"], d["wt1"], d["bt1"], d["wt2"], d["bt2"], d["wt3"], out)
    r = run_bass_kernel_spmd(nc, [{f"in_{n}": x for n, x in arrays.items()}], core_ids=[0])
    return r.results[0]["out"]
```
